# Optimizing a Trainium2 kernel written in Bass

```python
import numpy as np
import jax
import jax.numpy as jnp

def _softmax(x, axis=-1):
    return jax.nn.softmax(x, axis=axis)

def _gelu(x):
    return jax.nn.gelu(x, approximate=True)

def _silu(x):
    return jax.nn.silu(x)

def _sigmoid(x):
    return jax.nn.sigmoid(x)

def _layernorm(x, axis=-1, eps=1e-05):
    m = jnp.mean(x, axis=axis, keepdims=True)
    v = jnp.var(x, axis=axis, keepdims=True)
    return (x - m) / jnp.sqrt(v + eps)

def _scatter_add(tgt, idx, src, axis=0):
    return tgt.at[idx].add(src)

def _segment_sum(src, seg, n):
    return jax.ops.segment_sum(src, seg, n)
kernel_name = 'mk_gnn_preln_d1_gnn_r32_1899c2'

def setup_inputs(seed: int=0):
    np.random.seed(seed)
    _w = jnp.asarray

    def _rec_inputs():
        import jax
        import jax.numpy as jnp
        _gk = jax.random.key(seed)
        x = -0.0006008 + 1.001 * jax.random.normal(jax.random.fold_in(_gk, 1), (3125, 256), jnp.float32)
        _s = jax.random.randint(jax.random.fold_in(_gk, 2), (25000,), 0, 3125, jnp.int32)
        _d = jax.random.randint(jax.random.fold_in(_gk, 3), (25000,), 0, 3125, jnp.int32)
        _loop = jnp.arange(3125, dtype=jnp.int32)
        src = jnp.concatenate([_s, _d, _loop])
        dst = jnp.concatenate([_d, _s, _loop])
        _o = jnp.argsort(dst, stable=True)
        src = src[_o]
        dst = dst[_o]
        edge_attr_16 = 0.000130101 + 1.00012 * jax.random.normal(jax.random.fold_in(_gk, 11), (53125, 16), jnp.float32)
        return (x, src, dst, edge_attr_16)
    x, src, dst, edge_attr_16 = _rec_inputs()

    def _L0_gnn_setup():
        import jax, jax.numpy as jnp
        import numpy as np
        N, NODE_DIM, EDGE_DIM, HIDDEN, E = (10000, 256, 16, 512, 10000)
        key = jax.random.key(seed)
        ks = jax.random.split(key, 12)

        def lin(kw, kb, fan_in, fan_out):
            bound = 1.0 / np.sqrt(fan_in)
            W = jax.random.uniform(kw, (fan_in, fan_out), jnp.float32, -bound, bound)
            b = jax.random.uniform(kb, (fan_out,), jnp.float32, -bound, bound)
            return (W, b)
        node_features = jax.random.normal(ks[0], (N, NODE_DIM), jnp.float32)
        edge_index = jax.random.randint(ks[1], (2, E), 0, N, jnp.int32)
        edge_features = jax.random.normal(ks[2], (E, EDGE_DIM), jnp.float32)
        mW1, mb1 = lin(ks[3], ks[4], 2 * NODE_DIM + EDGE_DIM, HIDDEN)
        mW2, mb2 = lin(ks[5], ks[6], HIDDEN, NODE_DIM)
        uW1, ub1 = lin(ks[7], ks[8], 2 * NODE_DIM, HIDDEN)
        uW2, ub2 = lin(ks[9], ks[10], HIDDEN, NODE_DIM)
        return {'node_features': node_features, 'edge_index': edge_index, 'edge_features': edge_features, 'mW1': mW1, 'mb1': mb1, 'mW2': mW2, 'mb2': mb2, 'uW1': uW1, 'ub1': ub1, 'uW2': uW2, 'ub2': ub2}
    _L0_gnn_all = _L0_gnn_setup()
    _L0_gnn_in = {k: v for k, v in _L0_gnn_all.items() if k in ('mW1', 'mb1', 'mW2', 'mb2', 'uW1', 'ub1', 'uW2', 'ub2')}
    del _L0_gnn_all
    return {'x': x, 'src': src, 'dst': dst, 'edge_attr_16': edge_attr_16, 'L0_gnn_mW1': _L0_gnn_in['mW1'], 'L0_gnn_mb1': _L0_gnn_in['mb1'], 'L0_gnn_mW2': _L0_gnn_in['mW2'], 'L0_gnn_mb2': _L0_gnn_in['mb2'], 'L0_gnn_uW1': _L0_gnn_in['uW1'], 'L0_gnn_ub1': _L0_gnn_in['ub1'], 'L0_gnn_uW2': _L0_gnn_in['uW2'], 'L0_gnn_ub2': _L0_gnn_in['ub2']}

def reference(x, src, dst, edge_attr_16, L0_gnn_mW1, L0_gnn_mb1, L0_gnn_mW2, L0_gnn_mb2, L0_gnn_uW1, L0_gnn_ub1, L0_gnn_uW2, L0_gnn_ub2):
    import jax
    import jax.numpy as jnp

    def _L0_gnn_ref(node_features, edge_index, edge_features, mW1, mb1, mW2, mb2, uW1, ub1, uW2, ub2):
        import jax, jax.numpy as jnp
        import numpy as np
        N, NODE_DIM, EDGE_DIM, HIDDEN, E = (10000, 256, 16, 512, 10000)
        i_idx = edge_index[0]
        j_idx = edge_index[1]
        node_i = node_features[i_idx]
        node_j = node_features[j_idx]
        msg_input = jnp.concatenate([node_i, node_j, edge_features], axis=-1)
        h = jax.nn.relu(msg_input @ mW1 + mb1)
        messages = h @ mW2 + mb2
        aggregated = jax.ops.segment_sum(messages, i_idx, num_segments=node_features.shape[0])
        update_input = jnp.concatenate([node_features, aggregated], axis=-1)
        u = jax.nn.relu(update_input @ uW1 + ub1)
        updated = u @ uW2 + ub2
        return node_features + updated
    edge_index = jnp.stack([src, dst])
    h = jnp.maximum(_layernorm(x, axis=-1), 0.0)
    x = x + _L0_gnn_ref(h, edge_index, edge_attr_16, L0_gnn_mW1, L0_gnn_mb1, L0_gnn_mW2, L0_gnn_mb2, L0_gnn_uW1, L0_gnn_ub1, L0_gnn_uW2, L0_gnn_ub2)
    return x

_drawn_inputs = setup_inputs


def setup_inputs(seed=0):
    import zlib

    import numpy as np

    out = dict(_drawn_inputs(seed))
    spreads = {}
    factors = {'edge_attr_16': 3.414, 'L0_gnn_mb1': 4.067, 'L0_gnn_ub1': 8.0, 'L0_gnn_ub2': 3.476}
    for name, (base, spread) in spreads.items():
        noise = np.random.default_rng([zlib.crc32(name.encode()), seed]).standard_normal(out[name].shape)
        drawn = base * np.exp(spread * noise) if base else spread * noise
        out[name] = jnp.asarray(drawn.astype(out[name].dtype))
    for name, factor in factors.items():
        out[name] = (out[name] * factor).astype(out[name].dtype)
    return out
```

```python
import concourse.bass as bass
from concourse import mybir
from contextlib import ExitStack


def gnn_layer_kernel(nc, x, src, dst, edge_attr, mW1, mb1, mW2, mb2, uW1, ub1, uW2, ub2, out):
    f32, f32r, bf16, i32 = mybir.dt.float32, mybir.dt.float32r, mybir.dt.bfloat16, mybir.dt.int32
    ALU = mybir.AluOpType
    ACT = mybir.ActivationFunctionType
    AX = mybir.AxisListType
    ds = bass.ds

    N, D = x.shape
    E, DE = edge_attr.shape
    H = mW1.shape[1]
    NP = 125
    NT = N // NP
    EC = E // NP
    KD = D // 128
    KH = H // 128
    PAIR = 256
    NPAIR = (E + NT * (PAIR - 1)) // PAIR
    NPAIR += -NPAIR % 4
    NTILE = 2 * NPAIR
    BC = EC // NT
    NSLOT = 8
    REC = 2 + NSLOT * DE // 2
    RING = 4
    W1 = H + 1
    EPS = 1e-5
    ROUND = 12582912.0
    assert NP * NT == N and NP * EC == E and BC * NT == EC and NT % 2 == 1 and NPAIR % RING == 0

    records = nc.dram_tensor("records", (128 * NTILE, REC), f32).ap()
    B_dram = nc.dram_tensor("B_dram", (N, H), f32).ap()
    U_dram = nc.dram_tensor("U_dram", (NT, 128, KH * NP), f32).ap()
    xh_dram = nc.dram_tensor("xh_dram", (NT, NP, D), f32).ap()

    ctx = ExitStack()
    with ctx:
        def sb(name, shape, dt=f32):
            return ctx.enter_context(nc.sbuf_tensor(name, shape, dt))

        def sem(name):
            return ctx.enter_context(nc.semaphore(name))

        def carver(flat):
            used = [0]

            def carve(rows, words):
                used[0] += words
                assert used[0] <= flat.shape[1]
                return flat[0:rows, used[0] - words:used[0]]
            return carve

        A_hi = sb("A_hi", [NP, NT, H], f32r)
        A_lo = sb("A_lo", [NP, NT, H], f32r)
        hi_f = A_hi[:, :, :].bitcast(f32).rearrange("p t h -> p (t h)")
        lo_f = A_lo[:, :, :].bitcast(f32).rearrange("p t h -> p (t h)")
        run_f, hot_f = hi_f[:, 0:NT * EC], lo_f[:, 0:NT * EC]
        run = run_f.rearrange("p (a c) -> p a c", c=EC)
        hot = hot_f.rearrange("p (a c) -> p a c", c=EC)
        pb_tmp = hi_f[0:1, 0:(NT - 1) * NPAIR].rearrange("p (a j) -> p a j", j=NPAIR)
        xh_all = lo_f[:, 0:NT * D].rearrange("p (t d) -> p t d", d=D)

        w_src = sb("w_src", [128, KD, H])
        w_dst = sb("w_dst", [128, KD, H])
        w_node = sb("w_node", [128, KD, H])
        w_agg = w_dst
        w_msg2 = w_src[:, :, :].rearrange("p k (a d) -> p (k a) d", d=D)
        w_out = w_node[:, :, :].rearrange("p k (a d) -> p (k a) d", d=D)
        w_edge = sb("w_edge", [128, H], bf16)
        bias2 = sb("bias2", [1, 2 * D])
        iota1 = sb("iota1", [128, 128])
        iota1b = sb("iota1b", [128, 128], bf16)
        part1 = sb("part1", [128, 1])
        ident = sb("ident", [128, 128])
        identb = sb("identb", [128, 128], bf16)
        before = sb("before", [NP, NP])
        ones = sb("ones", [128, 128])
        epsc = sb("epsc", [128, 1])
        pair_bucket = sb("pair_bucket", [1, NPAIR], i32)

        S = sb("S", [128, NT, W1])
        S_flat = S[:, :, :].rearrange("p t w -> p (t w)")
        carve = carver(S_flat)
        x_all = carve(NP, NT * D).rearrange("p (t d) -> p t d", d=D)
        src_i = carve(NP, EC).bitcast(i32)
        dst_i = carve(NP, EC).bitcast(i32)
        place = carve(NP, EC).bitcast(i32)
        place_f = carve(NP, EC)
        local1 = carve(NP, EC)
        bucket = carve(NP, EC)
        small = carve(NP, 6 * NT).rearrange("p (k a) -> p k a", a=NT)
        small_i = carve(NP, NT).bitcast(i32)
        pair_iota = carve(1, NPAIR)
        bias1 = carve(1, 2 * H)
        h_t = carve(NP, D)
        we = [carve(DE, H)] + [carve(DE, H // 2).bitcast(bf16) for _ in range(3)]

        mid = sb("mid", [128, RING * 2 * H])
        g = mid[:, :].rearrange("p (r u h) -> p r u h", r=RING, u=2)
        carve = carver(mid[:, :])
        zero = carve(128, 8 * REC)
        recb_f = carve(NP, 2 * BC * REC)
        recb = recb_f.rearrange("p (r c w) -> p r c w", r=2, c=BC)
        recb_i = recb_f.bitcast(i32).rearrange("p (r c w) -> p r c w", r=2, c=BC)
        recb_bf = recb_f.bitcast(bf16).rearrange("p (r c w) -> p r c w", r=2, c=BC)
        row_i = carve(NP, 2 * BC).bitcast(i32).rearrange("p (r c) -> p r c", r=2)
        ea = carve(NP, 2 * BC * DE).rearrange("p (r c d) -> p r c d", r=2, c=BC)
        carve = carver(mid[:, :])
        S_t = carve(NP, W1)
        ST = carve(128, KH * 128).rearrange("p (c n) -> p c n", n=128)
        cntT = carve(1, NP)
        aggT = carve(128, KD * 128).rearrange("p (k n) -> p k n", n=128)
        uT = carve(128, KH * NP)
        o_sb = carve(NP, D)
        U_t = carve(128, 2 * KH * NP).rearrange("p (b n) -> p b n", b=2)

        rec = sb("rec", [128, RING * 2 * REC])
        rec_f = rec[:, :].rearrange("p (r u w) -> p r u w", r=RING, u=2)
        rec_i = rec[:, :].bitcast(i32).rearrange("p (r u w) -> p r u w", r=RING, u=2)
        rec_bf = rec[:, :].bitcast(bf16).rearrange("p (r u w) -> p r u w", r=RING, u=2)
        sel = sb("sel", [128, RING, 2, 128])
        selb = sb("selb", [128, RING, 2, 128], bf16)
        selT = sb("selT", [128, 2, 2, 128], f32r)
        eT = sb("eT", [128, 2, 2, 128], bf16)
        hid = sb("hid", [128, 2, 2, H])
        hT = hid[:, 0, 0, 0:KD * 128].rearrange("p (k n) -> p k n", n=128)
        B_sb = hid[0:NP, 0, 1, :]
        U_sb = hid[:, 1, 0, 0:KH * NP]
        stat = hid[0:NP, 1, 1, 0:16]

        ps = ctx.enter_context(nc.psum_tensor("ps", [128, 8, 512], f32))
        z_ps = ps[:, 0:2, :]
        S_ps = [ps[0:NP, 2 + 2 * b:4 + 2 * b, :].rearrange("p b n -> p (b n)") for b in range(2)]
        tr_ps = [ps[:, 6 + b, :].bitcast(bf16).rearrange("p (k n) -> p k n", n=128) for b in range(2)]

        ids_loaded, x_loaded, w_loaded, we_loaded = sem("ids_loaded"), sem("x_loaded"), sem("w_loaded"), sem("we_loaded")
        we_split, we_placed, w3_loaded = sem("we_split"), sem("we_placed"), sem("w3_loaded")
        ea_loaded = [sem(f"ea_loaded{r}") for r in range(2)]
        zero_set, zeroed, iota_set, const_set = sem("zero_set"), sem("zeroed"), sem("iota_set"), sem("const_set")
        chain = sem("chain")
        counts_set, counts_summed, order_done = sem("counts_set"), sem("counts_summed"), sem("order_done")
        e1_set, r1_set, e2_set, rec_built = sem("e1_set"), sem("r1_set"), sem("e2_set"), sem("rec_built")
        scattered = [sem(f"scattered{r}") for r in range(2)]
        norm_step, std_set, h_set, xh_set = sem("norm_step"), sem("std_set"), sem("h_set"), sem("xh_set")
        hT_done, B_done, A_done, U_done = sem("hT_done"), sem("B_done"), sem("A_done"), sem("U_done")
        hT_set, B_set, A_hi_set, A_lo_set, U_set = (sem("hT_set"), sem("B_set"), sem("A_hi_set"), sem("A_lo_set"),
                                                    sem("U_set"))
        B_stored, U_stored, xh_stored, S_zeroed = sem("B_stored"), sem("U_stored"), sem("xh_stored"), sem("S_zeroed")
        rec_loaded = [sem(f"rec_loaded{r}") for r in range(RING)]
        gathered = [[sem(f"gathered{r}_{u}") for u in range(2)] for r in range(RING)]
        sel_set, transposed, lhs_set = sem("sel_set"), sem("transposed"), sem("lhs_set")
        z_done, z_summed, hid_set, pair_done, S_added = (sem("z_done"), sem("z_summed"), sem("hid_set"),
                                                         sem("pair_done"), sem("S_added"))
        xh_loaded = sem("xh_loaded")
        U_loaded = [sem(f"U_loaded{b}") for b in range(2)]
        S_t_set, ST_done, ST_set, cnt_set = sem("S_t_set"), sem("ST_done"), sem("ST_set"), sem("cnt_set")
        agg_done, agg_set, u_done, u_summed, u_set = (sem("agg_done"), sem("agg_set"), sem("u_done"),
                                                      sem("u_summed"), sem("u_set"))
        o_done, o_set, o_stored = sem("o_done"), sem("o_set"), sem("o_stored")

        nop_engines = []
        block = ctx.enter_context(nc.Block())

        def wait(eng, s, n):
            if isinstance(n, int):
                if n > 0:
                    eng.wait_ge(s, n)
            else:
                eng.wait_ge(s, n)
                if eng in nop_engines:
                    eng.nop(nofuse=True)

        def over_blocks(eng, step):
            for t in range(3):
                step(t, t % 2, t // 2)
            with eng.Fori(1, NT // 2 - 1) as i:
                step(2 * i + 1, 1, i)
                step(2 * i + 2, 0, i + 1)
            for t in range(NT - 2, NT):
                step(t, t % 2, t // 2)

        def over_pairs(eng, step):
            for j in range(RING):
                step(j, j, 0)
            with eng.Fori(1, NPAIR // RING - 1) as i:
                for s in range(RING):
                    step(RING * i + s, s, i)
            for j in range(NPAIR - RING, NPAIR):
                step(j, j % RING, j // RING)

        def is_last(j, n):
            return isinstance(j, int) and j >= n

        @block.sync
        def _(sp):
            nop_engines.append(sp)
            sp.dma_start(src_i, src.rearrange("(p c) -> p c", c=EC)).then_inc(ids_loaded, 16)
            sp.dma_start(dst_i, dst.rearrange("(p c) -> p c", c=EC)).then_inc(ids_loaded, 16)
            sp.dma_start(x_all, x.rearrange("(t p) d -> p t d", p=NP)).then_inc(x_loaded, 16)
            sp.dma_start(we[0], mW1[2 * D:2 * D + DE, :]).then_inc(we_loaded, 16)
            for w, m in ((w_src, mW1[0:D, :]), (w_dst, mW1[D:2 * D, :]), (w_node, uW1[0:D, :])):
                sp.dma_start(w[:, :, :], m.rearrange("(k p) h -> p k h", p=128)).then_inc(w_loaded, 16)
            for row, b, n in ((bias1[:, 0:H], mb1, H), (bias1[:, H:2 * H], ub1, H), (bias2[:, 0:D], mb2, D),
                              (bias2[:, D:2 * D], ub2, D)):
                sp.dma_start(row, b.rearrange("(o h) -> o h", o=1)).then_inc(w_loaded, 16)
            sp.wait_ge(zero_set, 1)
            sp.dma_start(records.rearrange("(p b c) w -> p b (c w)", p=128, c=8),
                         zero.rearrange("p (o w) -> p o w", o=1).to_broadcast([128, NTILE // 8, 8 * REC])
                         ).then_inc(zeroed, 16)
            sp.wait_ge(we_split, 1)
            for k in range(NSLOT):
                sp.dma_start(w_edge[k * DE:(k + 1) * DE, :], we[1 + k % 3]).then_inc(we_placed, 16)

            ea_v = edge_attr.rearrange("(p b c) d -> p b (c d)", b=NT, c=BC)

            def load_edges(t, r, n):
                wait(sp, rec_built, t - 1)
                sp.dma_start(ea[:, r, :, :].rearrange("p c d -> p (c d)"),
                             ea_v[:, ds(t, 1), :].rearrange("p b w -> p (b w)")).then_inc(ea_loaded[r], 16)

            over_blocks(sp, load_edges)

            sp.wait_ge(U_done, NT)
            for w, m in ((w_agg[:, :, :], uW1[D:2 * D, :]), (w_msg2, mW2), (w_out, uW2)):
                sp.dma_start(w, m.rearrange("(k p) h -> p k h", p=128)).then_inc(w3_loaded, 16)
            for r in range(2):
                sp.wait_ge(scattered[r], 16 * BC * (NT // 2 + 1 - r))

            rec_v = records.rearrange("(p c) w -> p (c w)", c=NTILE)

            def load_records(j, s, n):
                wait(sp, transposed, j - RING + 1)
                wait(sp, z_summed, 2 * (j - RING + 1))
                sp.dma_start(rec[:, s * 2 * REC:(s + 1) * 2 * REC],
                             rec_v[:, ds(2 * REC * j, 2 * REC)]).then_inc(rec_loaded[s], 16)

            over_pairs(sp, load_records)

            sp.wait_ge(z_done, 2 * NPAIR)
            sp.wait_ge(xh_stored, 16)
            sp.dma_start(xh_all, xh_dram.rearrange("t p d -> p t d")).then_inc(xh_loaded, 16)
            sp.wait_ge(hid_set, 2 * NPAIR)
            sp.wait_ge(U_stored, 16 * NT)

            def load_U(t, r, n):
                wait(sp, u_set, t - 1)
                sp.dma_start(U_t[:, r, :], U_dram[ds(t, 1), :, :].rearrange("t p n -> p (t n)")).then_inc(U_loaded[r], 16)

            over_blocks(sp, load_U)

        @block.gpsimd
        def _(pool):
            nop_engines.append(pool)
            nc.gpsimd.memset(zero, 0.0).then_inc(zero_set, 1)
            for out_ap, pattern, base, mult in ((iota1[:, :], [[1, 128]], 1, 0), (part1[:, :], [[0, 1]], 1, 1),
                                                (pair_iota, [[1, NPAIR]], 0, 0)):
                nc.gpsimd.iota(out_ap, pattern=pattern, base=base, channel_multiplier=mult,
                               allow_small_or_imprecise_dtypes=True).then_inc(iota_set, 1)
            pool.wait_ge(zeroed, 16)

            def scatter(t, r, n):
                wait(pool, rec_built, t + 1)
                for k in range(BC):
                    nc.gpsimd.indirect_dma_start(
                        records[:, :], bass.IndirectOffsetOnAxis(ap=row_i[:, r, k:k + 1], axis=0),
                        recb[:, r, k, :], None).then_inc(scattered[r], 16)

            over_blocks(pool, scatter)
            for r in range(2):
                pool.wait_ge(scattered[r], 16 * BC * (NT // 2 + 1 - r))
            pool.wait_ge(B_stored, 16 * NT)

            def gather(j, s, n):
                wait(pool, rec_loaded[s], 16 * n + 16)
                for u in range(2):
                    wait(pool, hid_set, 2 * (j - RING) + u + 1)
                    nc.gpsimd.indirect_dma_start(
                        g[:, s, u, :], None, B_dram[:, :],
                        bass.IndirectOffsetOnAxis(ap=rec_i[:, s, u, 0:1], axis=0)).then_inc(gathered[s][u], 16)

            over_pairs(pool, gather)

        @block.scalar
        def _(act):
            a = nc.scalar
            act.wait_ge(const_set, 1)
            act.wait_ge(zeroed, 16)

            def step(t, r, n):
                slots = recb_bf[:, r, :, 4:].rearrange("p c (k d) -> p c k d", d=DE)
                e = ea[:, r, :, :].rearrange("p c (o d) -> p c o d", o=1).to_broadcast([NP, BC, 3, DE])
                wait(act, ea_loaded[r], 16 * n + 16)
                wait(act, scattered[r], 16 * BC * n)
                a.copy(slots[:, :, 0:3, :], e).then_inc(e1_set, 1)
                wait(act, r1_set, t + 1)
                a.copy(slots[:, :, 3:6, :], e).then_inc(e2_set, 1)
                wait(act, norm_step, 3 * t + 2)
                a.activation(stat[:, 8:9], stat[:, 7:8], ACT.Sqrt, bias=epsc[0:NP, :]).then_inc(std_set, 1)
                wait(act, hT_done, t + 1)
                wait(act, U_done, t)
                a.copy(hT[:, :, 0:NP], ps[:, 0, 0:KD * 128].rearrange("p (k n) -> p k n", n=128)[:, :, 0:NP]
                       ).then_inc(hT_set, 1)
                wait(act, B_done, t + 1)
                wait(act, B_stored, 16 * t)
                a.copy(B_sb, ps[0:NP, 1, :]).then_inc(B_set, 1)
                wait(act, B_set, t + 1)
                act.dma_start(B_dram.rearrange("(t p) h -> p t h", p=NP)[:, ds(t, 1), :],
                              B_sb.rearrange("p (t h) -> p t h", t=1)).then_inc(B_stored, 16)
                wait(act, A_done, t + 1)
                a.copy(A_hi[:, ds(t, 1), :], ps[0:NP, 2:3, :]).then_inc(A_hi_set, 1)
                wait(act, U_done, t + 1)
                wait(act, U_stored, 16 * t)
                a.copy(U_sb, ps[:, 3, 0:KH * NP]).then_inc(U_set, 1)
                wait(act, U_set, t + 1)
                act.dma_start(U_dram[ds(t, 1), :, :].rearrange("t p n -> p (t n)"), U_sb).then_inc(U_stored, 16)

            over_blocks(act, step)
            act.wait_ge(xh_set, NT)
            act.dma_start(xh_dram.rearrange("t p d -> p t d"), x_all).then_inc(xh_stored, 16)
            act.wait_ge(U_stored, 16 * NT)
            act.wait_ge(B_stored, 16 * NT)

            def evacuate(j):
                wait(act, transposed, j + 1)
                wait(act, z_done, 2 * (j - 1))
                b = evacuate.buffer
                evacuate.buffer = 1 - b
                a.copy(selT[:, b, :, :], tr_ps[b][:, 0:2, :])
                a.copy(eT[:, b, :, :], tr_ps[b][:, 2:4, :]).then_inc(lhs_set, 1)

            def relu(j, s, u):
                wait(act, z_summed, 2 * j + u + 1)
                wait(act, pair_done, j - 1)
                a.activation(hid[:, s % 2, u, :], g[:, s, u, :], ACT.Relu).then_inc(hid_set, 1)

            def pair(j, s, n):
                relu(j, s, 0)
                if not is_last(j, NPAIR - 1):
                    evacuate(j + 1)
                relu(j, s, 1)

            evacuate.buffer = 0
            evacuate(0)
            over_pairs(act, pair)

            def finish(t, r, n):
                wait(act, ST_done, t + 1)
                wait(act, agg_done, t)
                a.copy(ST[:, :, 0:NP], ps[:, 0, :].rearrange("p (c n) -> p c n", n=128)[:, :, 0:NP]).then_inc(ST_set, 1)
                wait(act, agg_done, t + 1)
                wait(act, u_done, t)
                a.copy(aggT[:, :, 0:NP], ps[:, 2, 0:KD * 128].rearrange("p (k n) -> p k n", n=128)[:, :, 0:NP]
                       ).then_inc(agg_set, 1)
                wait(act, u_summed, t + 1)
                wait(act, o_done, t)
                a.activation(uT, U_t[:, r, :], ACT.Relu).then_inc(u_set, 1)
                if not (isinstance(t, int) and t == 0):
                    store(t - 1)

            def store(t):
                wait(act, o_set, t + 1)
                act.dma_start(out.rearrange("(t p) d -> p t d", p=NP)[:, ds(t, 1), :],
                              o_sb.rearrange("p (t d) -> p t d", t=1)).then_inc(o_stored, 16)

            over_blocks(act, finish)
            store(NT - 1)
            act.wait_ge(o_stored, 16 * NT)

        @block.vector
        def _(dve):
            v = nc.vector
            steps = [0]

            def link(ins):
                steps[0] += 1
                ins.then_inc(chain, 1)
                dve.wait_ge(chain, steps[0])

            dve.wait_ge(iota_set, 3)
            dve.wait_ge(ids_loaded, 32)
            link(v.tensor_copy(local1, src_i))
            link(v.tensor_scalar(bucket, local1, 1.0 / NP, -(NP // 2) / NP, ALU.mult, ALU.add))
            link(v.tensor_scalar_add(bucket, bucket, ROUND))
            link(v.tensor_scalar_add(bucket, bucket, -ROUND))
            link(v.tensor_scalar_add(local1, local1, 1.0))
            link(v.scalar_tensor_tensor(local1, bucket, -float(NP), local1, ALU.mult, ALU.add))
            for m in (ident, identb):
                v.tensor_scalar(m[:, :], iota1[:, :], part1[:, :], None, ALU.is_equal)
            v.tensor_scalar(before[:, :], iota1[0:NP, 0:NP], part1[0:NP, :], None, ALU.is_gt)
            v.tensor_copy(iota1b[:, :], iota1[:, :])
            v.memset(epsc[:, :], EPS)
            v.memset(ones[:, :], 1.0).then_inc(const_set, 1)
            cum, cnt, pairs, ends, base = (small[:, k, :] for k in range(1, 6))
            link(v.tensor_scalar_add(small[:, 0, :], iota1[0:NP, 0:NT], -1.0))
            link(v.tensor_tensor(hot, bucket.rearrange("p (o c) -> p o c", o=1).to_broadcast([NP, NT, EC]),
                                 small[:, 0, :].rearrange("p (a o) -> p a o", o=1).to_broadcast([NP, NT, EC]),
                                 ALU.is_equal))
            link(v.tensor_tensor_scan(run_f, hot_f, hot_f, 0.0, ALU.add, ALU.max))
            link(v.tensor_copy(cum, run[:, :, EC - 1:EC].rearrange("p a o -> p (a o)")))
            link(v.tensor_copy(cnt[:, 0:1], cum[:, 0:1]))
            v.tensor_tensor(cnt[:, 1:NT], cum[:, 1:NT], cum[:, 0:NT - 1], ALU.subtract).then_inc(counts_set, 1)
            dve.wait_ge(counts_summed, 1)
            tot_ps, bef_ps = ps[0:NP, 0, 0:NT], ps[0:NP, 1, 0:NT]
            link(v.tensor_scalar_add(small_i, tot_ps, float(PAIR - 1)))
            link(v.tensor_scalar(small_i, small_i, 8, None, ALU.logical_shift_right))
            link(v.tensor_copy(pairs, small_i))
            link(v.tensor_tensor_scan(ends, pairs, pairs, 0.0, ALU.add, ALU.max))
            link(v.tensor_tensor(base, ends, pairs, ALU.subtract))
            link(v.scalar_tensor_tensor(base, base, float(PAIR), bef_ps, ALU.mult, ALU.add))
            link(v.tensor_scalar_add(base, base, -1.0))
            link(v.tensor_tensor(base[:, 1:NT], base[:, 1:NT], cum[:, 0:NT - 1], ALU.subtract))
            link(v.tensor_tensor(run, run, base.rearrange("p (a o) -> p a o", o=1).to_broadcast([NP, NT, EC]), ALU.add))
            link(v.tensor_tensor(run_f, run_f, hot_f, ALU.mult))
            link(v.tensor_reduce(place_f, run.rearrange("p a c -> p c a"), AX.X, ALU.add))
            link(v.tensor_copy(src_i, place_f))
            link(v.tensor_scalar(place, src_i, 127, None, ALU.bitwise_and))
            link(v.tensor_scalar(src_i, src_i, 7, None, ALU.logical_shift_right))
            link(v.scalar_tensor_tensor(place, place, float(NTILE), src_i, ALU.mult, ALU.add))
            link(v.tensor_tensor(
                pb_tmp, ends[0:1, 0:NT - 1].rearrange("p (a o) -> p a o", o=1).to_broadcast([1, NT - 1, NPAIR]),
                pair_iota.rearrange("p (o j) -> p o j", o=1).to_broadcast([1, NT - 1, NPAIR]), ALU.is_le))
            link(v.tensor_reduce(place_f[0:1, 0:NPAIR], pb_tmp.rearrange("p a j -> p j a"), AX.X, ALU.add))
            v.tensor_copy(pair_bucket[:, :], place_f[0:1, 0:NPAIR]).then_inc(order_done, 1)
            dve.wait_ge(we_loaded, 16)
            link(v.tensor_copy(we[1], we[0]))
            link(v.tensor_tensor(we[0], we[0], we[1], ALU.subtract))
            link(v.tensor_copy(we[2], we[0]))
            v.tensor_tensor(we[3], we[0], we[2], ALU.subtract).then_inc(we_split, 1)
            dve.wait_ge(x_loaded, 16)
            dve.wait_ge(zeroed, 16)

            def step(t, r, n):
                slots = recb_bf[:, r, :, 4:].rearrange("p c (k d) -> p c k d", d=DE)
                e = ea[:, r, :, :]
                wait(dve, scattered[r], 16 * BC * n)
                cols = ds(BC * t, BC)
                v.tensor_copy(recb_i[:, r, :, 0], dst_i[:, cols])
                v.tensor_copy(recb[:, r, :, 1], local1[:, cols])
                v.tensor_copy(row_i[:, r, :], place[:, cols])
                wait(dve, e1_set, t + 1)
                v.tensor_tensor(e, e, slots[:, :, 0, :], ALU.subtract).then_inc(r1_set, 1)
                wait(dve, e2_set, t + 1)
                v.tensor_tensor(
                    slots[:, :, 6:8, :], e.rearrange("p c (o d) -> p c o d", o=1).to_broadcast([NP, BC, 2, DE]),
                    slots[:, :, 3:4, :].to_broadcast([NP, BC, 2, DE]), ALU.subtract).then_inc(rec_built, 1)
                xt = x_all[:, ds(t, 1), :].rearrange("p t d -> p (t d)")
                v.bn_stats(stat[:, 0:6], xt).then_inc(norm_step, 1)
                wait(dve, norm_step, 3 * t + 1)
                dve.nop(nofuse=True)
                v.bn_aggr(stat[:, 6:8], stat[:, 0:6]).then_inc(norm_step, 1)
                wait(dve, std_set, t + 1)
                v.reciprocal(stat[:, 9:10], stat[:, 8:9]).then_inc(norm_step, 1)
                wait(dve, norm_step, 3 * t + 3)
                wait(dve, hT_done, t)
                v.tensor_scalar(h_t, xt, stat[:, 6:7], stat[:, 9:10], ALU.subtract, ALU.mult).then_inc(h_set, 1)
                wait(dve, h_set, 2 * t + 1)
                v.tensor_scalar_max(h_t, h_t, 0.0).then_inc(h_set, 1)
                wait(dve, h_set, 2 * t + 2)
                v.tensor_tensor(xt, xt, h_t, ALU.add).then_inc(xh_set, 1)
                wait(dve, A_hi_set, t + 1)
                v.tensor_tensor(A_lo[:, ds(t, 1), :], ps[0:NP, 2:3, :], A_hi[:, ds(t, 1), :].bitcast(f32),
                                ALU.subtract).then_inc(A_lo_set, 1)

            over_blocks(dve, step)

            dve.wait_ge(xh_stored, 16)
            dve.wait_ge(U_done, NT)
            dve.wait_ge(we_placed, 16 * NSLOT)
            for r in range(2):
                dve.wait_ge(scattered[r], 16 * BC * (NT // 2 + 1 - r))
            v.memset(S_flat, 0.0).then_inc(S_zeroed, 1)
            dve.wait_ge(S_zeroed, 1)

            def one_hots(j, s, n):
                wait(dve, rec_loaded[s], 16 * n + 16)
                wait(dve, pair_done, j - RING + 1)
                for u in range(2):
                    v.tensor_scalar(selb[:, s, u, :], iota1b[:, :], rec_f[:, s, u, 1:2], None, ALU.is_equal)
                    last = v.tensor_scalar(sel[:, s, u, :], iota1[:, :], rec_f[:, s, u, 1:2], None, ALU.is_equal)
                last.then_inc(sel_set, 1)

            def add_sums(j, s):
                k = v.value_load(pair_bucket[0:1, ds(j, 1)], min_val=0, max_val=NT - 1)
                row = S[0:NP, ds(k, 1), :].rearrange("p t w -> p (t w)")
                wait(dve, pair_done, j + 1)
                wait(dve, S_added, j)
                v.tensor_tensor(row, row, S_ps[s % 2][:, 0:W1], ALU.add).then_inc(S_added, 1)

            def pair(j, s, n):
                for u in range(2):
                    wait(dve, gathered[s][u], 16 * n + 16)
                    wait(dve, z_done, 2 * j + u + 1)
                    v.tensor_tensor(g[:, s, u, :], z_ps[:, u, :], g[:, s, u, :], ALU.add).then_inc(z_summed, 1)
                if not (isinstance(j, int) and j == 0):
                    add_sums(j - 1, (s - 1) % RING)
                if not is_last(j, NPAIR - 2):
                    one_hots(j + 2, (s + 2) % RING, n + (s + 2) // RING)

            one_hots(0, 0, 0)
            one_hots(1, 1, 0)
            over_pairs(dve, pair)
            add_sums(NPAIR - 1, RING - 1)

            dve.wait_ge(S_added, NPAIR)
            dve.wait_ge(hid_set, 2 * NPAIR)
            dve.wait_ge(xh_loaded, 16)

            def stage(t):
                wait(dve, ST_done, t)
                v.tensor_copy(S_t, S[0:NP, ds(t, 1), :].rearrange("p t w -> p (t w)")).then_inc(S_t_set, 1)

            def output(t):
                wait(dve, o_done, t + 1)
                wait(dve, o_stored, 16 * t)
                v.tensor_tensor(o_sb, ps[0:NP, 4, 0:D], xh_all[:, ds(t, 1), :].rearrange("p t d -> p (t d)"),
                                ALU.add).then_inc(o_set, 1)

            def finish(t, r, n):
                wait(dve, ST_done, t + 1)
                wait(dve, agg_done, t)
                v.tensor_copy(cntT, ps[0:1, 1, 0:NP]).then_inc(cnt_set, 1)
                if not is_last(t, NT - 1):
                    stage(t + 1)
                if not (isinstance(t, int) and t == 0):
                    output(t - 1)
                wait(dve, u_done, t + 1)
                wait(dve, U_loaded[r], 16 * n + 16)
                v.tensor_tensor(U_t[:, r, :], ps[:, 3, 0:KH * NP], U_t[:, r, :], ALU.add).then_inc(u_summed, 1)

            stage(0)
            over_blocks(dve, finish)
            output(NT - 1)

        @block.tensor
        def _(pe):
            mm = nc.tensor.matmul
            pe.wait_ge(const_set, 1)
            pe.wait_ge(counts_set, 1)
            cnt = small[:, 2, :]
            mm(ps[0:NP, 0, 0:NT], ones[0:NP, 0:NP], cnt, start=True, stop=True)
            mm(ps[0:NP, 1, 0:NT], before[:, :], cnt, start=True, stop=True).then_inc(counts_summed, 1)
            pe.wait_ge(w_loaded, 16 * 7)

            def step(t, r, n):
                wait(pe, h_set, 2 * t + 2)
                wait(pe, hT_set, t)
                for k in range(KD):
                    last = nc.tensor.transpose(ps[:, 0, k * 128:k * 128 + NP], h_t[:, k * 128:(k + 1) * 128],
                                               ident[0:NP, 0:NP])
                last.then_inc(hT_done, 1)
                wait(pe, hT_set, t + 1)
                wait(pe, B_set, t)
                for k in range(KD):
                    last = mm(ps[0:NP, 1, :], hT[:, k, 0:NP], w_dst[:, k, :], start=k == 0, stop=k == KD - 1)
                last.then_inc(B_done, 1)
                wait(pe, A_lo_set, t)
                for k in range(KD):
                    mm(ps[0:NP, 2, :], hT[:, k, 0:NP], w_src[:, k, :], start=k == 0, stop=False)
                mm(ps[0:NP, 2, :], ones[0:1, 0:NP], bias1[:, 0:H], start=False, stop=True).then_inc(A_done, 1)
                wait(pe, U_set, t)
                for c in range(KH):
                    o = ps[:, 3, c * NP:(c + 1) * NP]
                    for k in range(KD):
                        mm(o, w_node[:, k, c * 128:(c + 1) * 128], hT[:, k, 0:NP], start=k == 0, stop=False)
                    last = mm(o, bias1[:, H + c * 128:H + (c + 1) * 128], ones[0:1, 0:NP], start=False, stop=True)
                last.then_inc(U_done, 1)

            over_blocks(pe, step)
            pe.wait_ge(we_placed, 16 * NSLOT)
            pe.wait_ge(order_done, 1)
            pe.wait_ge(B_set, NT)
            pe.wait_ge(A_lo_set, NT)
            pe.wait_ge(U_set, NT)

            def transposes(j, s):
                wait(pe, sel_set, j + 1)
                wait(pe, lhs_set, j - 1)
                for u in range(2):
                    nc.tensor.transpose(tr_ps[s % 2][:, u, :], selb[:, s, u, :], identb[:, :])
                    last = nc.tensor.transpose(tr_ps[s % 2][:, 2 + u, :], rec_bf[:, s, u, 4:], identb[:, :])
                last.then_inc(transposed, 1)

            def pre_relu(j, s, u, k):
                wait(pe, lhs_set, j + 1)
                wait(pe, z_summed, 2 * (j - 1) + u + 1)
                b = s % 2
                for n, part in enumerate((A_hi, A_lo)):
                    mm(z_ps[:, u, :], selT[0:NP, b, u, :], part[:, ds(k, 1), :].rearrange("p t h -> p (t h)"),
                       start=n == 0, stop=False)
                mm(z_ps[:, u, :], eT[:, b, u, :], w_edge[:, :], start=False, stop=True).then_inc(z_done, 1)

            def sums(j, s, u):
                wait(pe, hid_set, 2 * j + u + 1)
                if u == 0:
                    wait(pe, S_added, j - 1)
                b = s % 2
                mm(S_ps[b][:, 0:H], sel[:, s, u, 0:NP], hid[:, b, u, :], start=u == 0, stop=u == 1)
                last = mm(S_ps[b][:, H:W1], sel[:, s, u, 0:NP], ones[:, 0:1], start=u == 0, stop=u == 1)
                if u == 1:
                    last.then_inc(pair_done, 1)

            def pair(j, s, n):
                first = isinstance(j, int) and j == 0
                k = nc.tensor.value_load(pair_bucket[0:1, ds(j, 1)], min_val=0, max_val=NT - 1)
                pre_relu(j, s, 0, k)
                if not is_last(j, NPAIR - 1):
                    transposes(j + 1, (s + 1) % RING)
                if not first:
                    sums(j - 1, (s - 1) % RING, 0)
                pre_relu(j, s, 1, k)
                if not first:
                    sums(j - 1, (s - 1) % RING, 1)

            transposes(0, 0)
            over_pairs(pe, pair)
            sums(NPAIR - 1, RING - 1, 0)
            sums(NPAIR - 1, RING - 1, 1)

            pe.wait_ge(w3_loaded, 48)
            pe.wait_ge(S_added, NPAIR)

            def output(t):
                wait(pe, u_set, t + 1)
                wait(pe, o_set, t)
                for c in range(KH):
                    mm(ps[0:NP, 4, 0:D], uT[:, c * NP:(c + 1) * NP], w_out[:, c, :], start=c == 0, stop=False)
                mm(ps[0:NP, 4, 0:D], ones[0:1, 0:NP], bias2[:, D:2 * D], start=False, stop=True).then_inc(o_done, 1)

            def finish(t, r, n):
                wait(pe, S_t_set, t + 1)
                wait(pe, ST_set, t)
                wait(pe, cnt_set, t)
                for c in range(KH):
                    nc.tensor.transpose(ps[:, 0, c * 128:c * 128 + NP], S_t[:, c * 128:(c + 1) * 128],
                                        ident[0:NP, 0:NP])
                nc.tensor.transpose(ps[0:1, 1, 0:NP], S_t[:, H:W1], ident[0:NP, 0:NP]).then_inc(ST_done, 1)
                if not (isinstance(t, int) and t == 0):
                    output(t - 1)
                wait(pe, ST_set, t + 1)
                wait(pe, cnt_set, t + 1)
                wait(pe, agg_set, t)
                for k in range(KD):
                    o = ps[:, 2, k * 128:k * 128 + NP]
                    for c in range(KH):
                        mm(o, w_msg2[:, c, k * 128:(k + 1) * 128], ST[:, c, 0:NP], start=c == 0, stop=False)
                    last = mm(o, bias2[:, k * 128:(k + 1) * 128], cntT, start=False, stop=True)
                last.then_inc(agg_done, 1)
                wait(pe, agg_set, t + 1)
                wait(pe, u_summed, t)
                for c in range(KH):
                    for k in range(KD):
                        last = mm(ps[:, 3, c * NP:(c + 1) * NP], w_agg[:, k, c * 128:(c + 1) * 128], aggT[:, k, 0:NP],
                                  start=k == 0, stop=k == KD - 1)
                last.then_inc(u_done, 1)

            over_blocks(pe, finish)
            output(NT - 1)


_INS = ['x', 'src', 'dst', 'edge_attr_16', 'L0_gnn_mW1', 'L0_gnn_mb1', 'L0_gnn_mW2', 'L0_gnn_mb2', 'L0_gnn_uW1',
        'L0_gnn_ub1', 'L0_gnn_uW2', 'L0_gnn_ub2']


def kernel(**inputs):
    import numpy as _np
    import concourse.bacc as _bacc
    from concourse import mybir as _mybir
    from concourse.bass_utils import run_bass_kernel_spmd as _run

    nc = _bacc.Bacc("TRN2", target_bir_lowering=False, num_devices=1)
    arrays, args = {}, []
    for name in _INS:
        a = _np.ascontiguousarray(inputs[name])
        arrays[f"in_{name}_dram"] = a
        args.append(nc.dram_tensor(f"in_{name}_dram", a.shape, _mybir.dt.from_np(a.dtype), kind="ExternalInput").ap())
    shape = inputs['x'].shape
    args.append(nc.dram_tensor("out_dram", shape, _mybir.dt.float32, kind="ExternalOutput").ap())
    gnn_layer_kernel(nc, *args)
    r = _run(nc, [arrays], core_ids=[0])
    return r.results[0]["out_dram"]
```

```python
import concourse.bass as bass
import numpy as np
from concourse import mybir
from contextlib import ExitStack


def gnn_layer_kernel(nc, x, src, dst, edge_attr, mW1, mb1, mW2, mb2, uW1, ub1, uW2, ub2, out):
    f32, f32r, bf16, i32 = mybir.dt.float32, mybir.dt.float32r, mybir.dt.bfloat16, mybir.dt.int32
    ALU = mybir.AluOpType
    ACT = mybir.ActivationFunctionType
    AX = mybir.AxisListType
    ds = bass.ds

    N, D = x.shape
    E, DE = edge_attr.shape
    H = mW1.shape[1]
    NP = 125
    NT = N // NP
    EC = E // NP
    KD = D // 128
    KH = H // 128
    PAIR = 256
    RING = 4
    UNROLL = 8
    NPAIR = (E + NT * (PAIR - 1)) // PAIR
    NPAIR += -NPAIR % UNROLL
    NTILE = 2 * NPAIR
    BC = EC // NT
    NSLOT = 8
    REC = 2 + NSLOT * DE // 2
    AHEAD = 3
    FIRST = 2
    EPS = 1e-5
    ROUND = 12582912.0
    assert NP * NT == N and NP * EC == E and BC * NT == EC and NT % 2 == 1

    records = nc.dram_tensor("records", (128 * NTILE, REC), f32).ap()
    B_dram = nc.dram_tensor("B_dram", (N, H), f32).ap()
    cnt_dram = nc.dram_tensor("cnt_dram", (NT, NP), f32).ap()
    U_dram = nc.dram_tensor("U_dram", (NT, 128, KH * NP), f32).ap()
    xh_dram = nc.dram_tensor("xh_dram", (NT, NP, D), f32).ap()

    ctx = ExitStack()
    with ctx:
        def sb(name, shape, dt=f32):
            return ctx.enter_context(nc.sbuf_tensor(name, shape, dt))

        def sem(name):
            return ctx.enter_context(nc.semaphore(name))

        def carver(flat):
            used = [0]

            def carve(rows, words):
                used[0] += words
                assert used[0] <= flat.shape[1]
                return flat[0:rows, used[0] - words:used[0]]
            return carve

        w_in = sb("w_in", [128, KH, H])
        w_src, w_dst = w_in[:, 0:KD, :], w_in[:, KD:KH, :]
        w_upd = w_in
        w_node = sb("w_node", [128, KD, H])
        w_out = w_node[:, :, :].rearrange("p k (a d) -> p (k a) d", d=D)
        w_edge = sb("w_edge", [128, H], bf16)
        q_upd = sb("q_upd", [128, KH])
        mb2_cols = sb("mb2_cols", [128, KD])
        iota1 = sb("iota1", [128, 128])
        part1 = sb("part1", [128, 1])
        ident = sb("ident", [128, 128])
        identb = sb("identb", [128, 128], bf16)
        ones = sb("ones", [128, 128])
        epsc = sb("epsc", [128, 1])
        pair_bucket = sb("pair_bucket", [1, NPAIR], i32)

        S = sb("S", [128, NT, H])
        S_flat = S[:, :, :].rearrange("p t w -> p (t w)")
        carve = carver(S_flat)
        x_all = carve(NP, NT * D).rearrange("p (t d) -> p t d", d=D)
        src_i = carve(NP, EC).bitcast(i32)
        dst_i = carve(NP, EC).bitcast(i32)
        place = carve(NP, EC).bitcast(i32)
        place_f = carve(NP, EC)
        local1 = carve(NP, EC)
        bucket = carve(NP, EC)
        small = carve(NP, 6 * NT).rearrange("p (k a) -> p k a", a=NT)
        small_i = carve(NP, NT).bitcast(i32)
        pair_iota = carve(NT, NPAIR)
        ended = carve(NT, NPAIR)
        ends_diag = carve(NT, NT)
        bias1 = carve(1, 2 * H)
        bias_out = carve(1, D)
        ub2_rows = carve(NP, D)
        before = carve(NP, NP)
        cnt_sb = carve(NP, NT)
        cntT_sb = carve(NT, NP)
        we = [carve(DE, H)] + [carve(DE, H // 2).bitcast(bf16) for _ in range(3)]

        mid = sb("mid", [128, RING * 2 * H])
        g = mid[:, :].rearrange("p (r u h) -> p r u h", r=RING, u=2)
        carve = carver(mid[:, :])
        zero = carve(128, 8 * REC)
        recb_f = carve(NP, 2 * BC * REC)
        recb = recb_f.rearrange("p (r c w) -> p r c w", r=2, c=BC)
        recb_i = recb_f.bitcast(i32).rearrange("p (r c w) -> p r c w", r=2, c=BC)
        recb_bf = recb_f.bitcast(bf16).rearrange("p (r c w) -> p r c w", r=2, c=BC)
        row_i = carve(NP, 2 * BC).bitcast(i32).rearrange("p (r c) -> p r c", r=2)
        ea = carve(NP, 2 * BC * DE).rearrange("p (r c d) -> p r c d", r=2, c=BC)
        carve = carver(mid[:, :])
        S_t = carve(NP, H)
        ST = carve(128, KH * 128).rearrange("p (c n) -> p c n", n=128)
        o_sb = carve(NP, D)
        U_t = carve(128, 2 * KH * NP).rearrange("p (b n) -> p b n", b=2)

        rec = sb("rec", [128, RING * 2 * REC])
        rec_f = rec[:, :].rearrange("p (r u w) -> p r u w", r=RING, u=2)
        rec_i = rec[:, :].bitcast(i32).rearrange("p (r u w) -> p r u w", r=RING, u=2)
        rec_bf = rec[:, :].bitcast(bf16).rearrange("p (r u w) -> p r u w", r=RING, u=2)
        hot_b = rec[0:NP, 0:(BC * NT + 1) // 2].bitcast(bf16)[:, 0:BC * NT].rearrange("p (c a) -> p c a", a=NT)
        selb = sb("selb", [128, 2, 2, 128], bf16)
        eT = sb("eT", [128, 2, 2, 128], bf16)
        hid = sb("hid", [128, 2, H])
        hT = hid[:, 0, 0:KD * 128].rearrange("p (k n) -> p k n", n=128)
        stat = hid[0:NP, 0, KD * 128:KD * 128 + 16]
        h_t = hid[0:NP, 1, 0:D]

        def sharing(name, *sets):
            for tensors in sets:
                with ExitStack() as one:
                    yield [one.enter_context(nc.sbuf_tensor(*t)) for t in tensors]
            sb(name, [128, max(sum(int(np.prod(shape[1:])) for _, shape, _ in tensors) for tensors in sets)])

        spare = NT * (H - EC)
        (run_t, hot_t), (A_hi, A_lo), (late1, late2) = sharing(
            "kept1", (("run_t", [NP, NT * H], f32), ("hot_t", [NP, NT * H], f32)),
            (("A_hi", [NP, NT, H], f32r), ("A_lo", [NP, NT, H], f32r)),
            (("late1", [128, NT * H], f32), ("late2", [128, NT * H], f32)))
        run_f, hot_f = run_t[:, spare:], hot_t[:, spare:]
        run = run_f.rearrange("p (a c) -> p a c", c=EC)
        hot = hot_f.rearrange("p (a c) -> p a c", c=EC)
        xh_all = late1[0:NP, 0:NT * D].rearrange("p (t d) -> p t d", d=D)
        cnt_rows = late2[:, 0:N]
        (tiles,), (sel, selT, hid_hi, hid_lo) = sharing(
            "kept2", (("tiles", [128, (4 + KD) * H], f32),),
            (("sel", [128, RING, 2, 128], f32r), ("selT", [128, 2, 2, 128], f32r),
             ("hid_hi", [128, 2, H], f32r), ("hid_lo", [128, 2, H], f32r)))
        B_sb = tiles[0:NP, 0:H]
        U_sb = tiles[:, H:H + KH * NP]
        hot_n = tiles[0:NP, 2 * H:2 * H + (BC * NP + 1) // 2].bitcast(bf16)[:, 0:BC * NP].rearrange(
            "p (c n) -> p c n", n=NP)
        w_agg = tiles[:, 0:KD * H].rearrange("p (k h) -> p k h", k=KD)
        w_msg2 = tiles[:, KD * H:4 * H].rearrange("p (k d) -> p k d", d=D)
        m2T = tiles[:, 4 * H:].rearrange("p (k h) -> p k h", k=KD)

        ps = ctx.enter_context(nc.psum_tensor("ps", [128, 8, 512], f32))
        z_ps = ps[:, 0:2, :]
        S_ps = [ps[0:NP, 2 + b, :] for b in range(2)]
        tr_ps = [ps[:, 6 + b, :].bitcast(bf16).rearrange("p (k n) -> p k n", n=128) for b in range(2)]

        ids_loaded, x_loaded, w_loaded, we_loaded = sem("ids_loaded"), sem("x_loaded"), sem("w_loaded"), sem("we_loaded")
        we_split, we_placed, w3_loaded = sem("we_split"), sem("we_placed"), sem("w3_loaded")
        ea_loaded = [sem(f"ea_loaded{r}") for r in range(2)]
        zero_set, zeroed, iota_set, const_set = sem("zero_set"), sem("zeroed"), sem("iota_set"), sem("const_set")
        chain = sem("chain")
        counts_set, counts_summed, order_done = sem("counts_set"), sem("counts_summed"), sem("order_done")
        ended_set, buckets_counted = sem("ended_set"), sem("buckets_counted")
        hot_set, hot_used, cnt_stored = sem("hot_set"), sem("hot_used"), sem("cnt_stored")
        e1_set, r1_set, e2_set, rec_built = sem("e1_set"), sem("r1_set"), sem("e2_set"), sem("rec_built")
        scattered = [sem(f"scattered{r}") for r in range(2)]
        norm_step, std_set, h_set, xh_set = sem("norm_step"), sem("std_set"), sem("h_set"), sem("xh_set")
        hT_done, B_done, A_done, U_done = sem("hT_done"), sem("B_done"), sem("A_done"), sem("U_done")
        hT_set, B_set, A_hi_set, A_lo_set, U_set = (sem("hT_set"), sem("B_set"), sem("A_hi_set"), sem("A_lo_set"),
                                                    sem("U_set"))
        B_stored, U_stored, xh_stored, S_zeroed = sem("B_stored"), sem("U_stored"), sem("xh_stored"), sem("S_zeroed")
        rec_loaded = [sem(f"rec_loaded{r}") for r in range(RING)]
        gathered = [[sem(f"gathered{r}_{u}") for u in range(2)] for r in range(RING)]
        sel_set, selb_set, transposed, lhs_set = sem("sel_set"), sem("selb_set"), sem("transposed"), sem("lhs_set")
        lo_set = sem("lo_set")
        z_done, z_summed, hid_set, pair_done, S_added = (sem("z_done"), sem("z_summed"), sem("hid_set"),
                                                         sem("pair_done"), sem("S_added"))
        xh_loaded = sem("xh_loaded")
        U_loaded = [sem(f"U_loaded{b}") for b in range(2)]
        m2T_done, m2T_set, upd_done, upd_set = sem("m2T_done"), sem("m2T_set"), sem("upd_done"), sem("upd_set")
        cnt_set, cntT_done, cntT_set = sem("cnt_set"), sem("cntT_done"), sem("cntT_set")
        ub2_done = sem("ub2_done")
        S_t_set, ST_done, ST_set, node_step = sem("S_t_set"), sem("ST_done"), sem("ST_set"), sem("node_step")
        u_done, u_summed, u_set = sem("u_done"), sem("u_summed"), sem("u_set")
        o_done, o_set, o_stored = sem("o_done"), sem("o_set"), sem("o_stored")

        nop_engines = []
        block = ctx.enter_context(nc.Block())

        def wait(eng, s, n):
            if isinstance(n, int):
                if n > 0:
                    eng.wait_ge(s, n)
            else:
                eng.wait_ge(s, n)
                if eng in nop_engines:
                    eng.nop(nofuse=True)

        def over_blocks(eng, step):
            for t in range(3):
                step(t, t % 2, t // 2)
            with eng.Fori(1, NT // 2 - 1) as i:
                step(2 * i + 1, 1, i)
                step(2 * i + 2, 0, i + 1)
            for t in range(NT - 2, NT):
                step(t, t % 2, t // 2)

        def next_build(build, t, r, n):
            if isinstance(t, int) and t < 2:
                build(t + 2, r, 1)
            elif not (isinstance(t, int) and t in (2, NT - 1)):
                build(t + 1, 1 - r, n + r)

        def over_pairs(eng, step):
            for j in range(RING):
                step(j, j, 0)
            with eng.Fori(0, (NPAIR - 2 * RING) // UNROLL) as i:
                for s in range(UNROLL):
                    step(UNROLL * i + RING + s, s % RING, UNROLL // RING * i + 1 + s // RING)
            for j in range(NPAIR - RING, NPAIR):
                step(j, j % RING, j // RING)

        def is_last(j, n):
            return isinstance(j, int) and j >= n

        @block.sync
        def _(sp):
            nop_engines.append(sp)
            sp.dma_start(src_i, src.rearrange("(p c) -> p c", c=EC)).then_inc(ids_loaded, 16)
            sp.dma_start(dst_i, dst.rearrange("(p c) -> p c", c=EC)).then_inc(ids_loaded, 16)
            ea_v = edge_attr.rearrange("(p b c) d -> p b (c d)", b=NT, c=BC)
            for r in range(2):
                sp.dma_start(ea[:, r, :, :].rearrange("p c d -> p (c d)"), ea_v[:, r, :]).then_inc(ea_loaded[r], 16)
            sp.wait_ge(zero_set, 1)
            sp.dma_start(records.rearrange("(p b c) w -> p b (c w)", p=128, c=8),
                         zero.rearrange("p (o w) -> p o w", o=1).to_broadcast([128, NTILE // 8, 8 * REC])
                         ).then_inc(zeroed, 16)

            def load_edges(t, r, n):
                if not (isinstance(t, int) and t < 2):
                    wait(sp, rec_built, t - 1)
                    sp.dma_start(ea[:, r, :, :].rearrange("p c d -> p (c d)"),
                                 ea_v[:, ds(t, 1), :].rearrange("p b w -> p (b w)")).then_inc(ea_loaded[r], 16)
                if isinstance(t, int) and t == 1:
                    sp.dma_start(x_all, x.rearrange("(t p) d -> p t d", p=NP)).then_inc(x_loaded, 16)
                    for w, m in ((w_src, mW1[0:D, :]), (w_dst, mW1[D:2 * D, :]), (w_node[:, :, :], uW1[0:D, :])):
                        sp.dma_start(w, m.rearrange("(k p) h -> p k h", p=128)).then_inc(w_loaded, 16)
                    for row, b in ((bias1[:, 0:H], mb1), (bias1[:, H:2 * H], ub1), (bias_out, ub2)):
                        sp.dma_start(row, b.rearrange("(o h) -> o h", o=1)).then_inc(w_loaded, 16)
                    for k in range(KD):
                        sp.dma_start(mb2_cols[:, k:k + 1], mb2[k * 128:(k + 1) * 128].rearrange("(p o) -> p o", o=1)
                                     ).then_inc(w_loaded, 16)
                    sp.dma_start(we[0], mW1[2 * D:2 * D + DE, :]).then_inc(we_loaded, 16)
                if isinstance(t, int) and t == 2:
                    sp.wait_ge(we_split, 1)
                    for k in range(NSLOT):
                        sp.dma_start(w_edge[k * DE:(k + 1) * DE, :], we[1 + k % 3]).then_inc(we_placed, 16)

            over_blocks(sp, load_edges)

            sp.wait_ge(U_done, NT)
            sp.wait_ge(B_stored, 16 * NT)
            sp.wait_ge(U_stored, 16 * NT)
            sp.wait_ge(hot_used, NT)
            for w, m in ((w_agg, uW1[D:2 * D, :]), (w_msg2, mW2), (w_out, uW2)):
                sp.dma_start(w, m.rearrange("(k p) h -> p k h", p=128)).then_inc(w3_loaded, 16)
            sp.wait_ge(cntT_set, 1)
            sp.dma_start(cnt_dram[:, :], cntT_sb).then_inc(cnt_stored, 16)
            for r in range(2):
                sp.wait_ge(scattered[r], 16 * BC * (NT // 2 + 1 - r))

            rec_v = records.rearrange("(p c) w -> p (c w)", c=NTILE)

            def load_records(j, s, n):
                wait(sp, transposed, j - RING + 1)
                wait(sp, z_summed, 2 * (j - RING + 1))
                sp.dma_start(rec[:, s * 2 * REC:(s + 1) * 2 * REC],
                             rec_v[:, ds(2 * REC * j, 2 * REC)]).then_inc(rec_loaded[s], 16)

            over_pairs(sp, load_records)

            sp.wait_ge(z_done, 2 * NPAIR)
            sp.wait_ge(xh_stored, 16)
            sp.dma_start(xh_all, xh_dram.rearrange("t p d -> p t d")).then_inc(xh_loaded, 16)
            sp.wait_ge(cnt_stored, 16)
            sp.dma_start(cnt_rows, cnt_dram.rearrange("(o t) p -> o (t p)", o=1).to_broadcast([128, N])
                         ).then_inc(xh_loaded, 16)
            sp.wait_ge(hid_set, 2 * NPAIR)
            sp.wait_ge(lo_set, NPAIR)

            def load_U(t, r, n):
                wait(sp, o_done, t - 1)
                sp.dma_start(U_t[:, r, :], U_dram[ds(t, 1), :, :].rearrange("t p n -> p (t n)")).then_inc(U_loaded[r], 16)

            over_blocks(sp, load_U)

        @block.gpsimd
        def _(pool):
            nop_engines.append(pool)
            nc.gpsimd.memset(zero, 0.0).then_inc(zero_set, 1)
            for out_ap, pattern, base, mult in ((iota1[:, :], [[1, 128]], 1, 0), (part1[:, :], [[0, 1]], 1, 1),
                                                (pair_iota, [[1, NPAIR]], 0, 0)):
                nc.gpsimd.iota(out_ap, pattern=pattern, base=base, channel_multiplier=mult,
                               allow_small_or_imprecise_dtypes=True).then_inc(iota_set, 1)
            pool.wait_ge(zeroed, 16)

            def scatter(t, r, n):
                wait(pool, rec_built, t + 1)
                for k in range(BC):
                    nc.gpsimd.indirect_dma_start(
                        records[:, :], bass.IndirectOffsetOnAxis(ap=row_i[:, r, k:k + 1], axis=0),
                        recb[:, r, k, :], None).then_inc(scattered[r], 16)

            over_blocks(pool, scatter)
            for r in range(2):
                pool.wait_ge(scattered[r], 16 * BC * (NT // 2 + 1 - r))
            pool.wait_ge(B_stored, 16 * NT)

            def gather(j, s, n):
                wait(pool, rec_loaded[s], 16 * n + 16)
                for u in range(2):
                    wait(pool, hid_set, 2 * (j - RING) + u + 1)
                    if u == 1:
                        wait(pool, lo_set, j - RING + 1)
                    nc.gpsimd.indirect_dma_start(
                        g[:, s, u, :], None, B_dram[:, :],
                        bass.IndirectOffsetOnAxis(ap=rec_i[:, s, u, 0:1], axis=0)).then_inc(gathered[s][u], 16)

            over_pairs(pool, gather)

        @block.scalar
        def _(act):
            a = nc.scalar
            act.wait_ge(const_set, 1)

            def build(t, r, n):
                slots = recb_bf[:, r, :, 4:].rearrange("p c (k d) -> p c k d", d=DE)
                e = ea[:, r, :, :].rearrange("p c (o d) -> p c o d", o=1).to_broadcast([NP, BC, 3, DE])
                wait(act, ea_loaded[r], 16 * n + 16)
                wait(act, scattered[r], 16 * BC * n)
                a.copy(slots[:, :, 0:3, :], e).then_inc(e1_set, 1)
                wait(act, r1_set, t + 1)
                a.copy(slots[:, :, 3:6, :], e).then_inc(e2_set, 1)

            def step(t, r, n):
                next_build(build, t, r, n)
                wait(act, norm_step, 3 * t + 2)
                a.activation(stat[:, 8:9], stat[:, 7:8], ACT.Sqrt, bias=epsc[0:NP, :]).then_inc(std_set, 1)
                wait(act, hT_done, t + 1)
                wait(act, U_done, t)
                a.copy(hT[:, :, 0:NP], ps[:, 0, 0:KD * 128].rearrange("p (k n) -> p k n", n=128)[:, :, 0:NP]
                       ).then_inc(hT_set, 1)
                wait(act, B_done, t + 1)
                wait(act, B_stored, 16 * t)
                a.copy(B_sb, ps[0:NP, 1, :]).then_inc(B_set, 1)
                wait(act, B_set, t + 1)
                act.dma_start(B_dram.rearrange("(t p) h -> p t h", p=NP)[:, ds(t, 1), :],
                              B_sb.rearrange("p (t h) -> p t h", t=1)).then_inc(B_stored, 16)
                wait(act, A_done, t + 1)
                a.copy(A_hi[:, ds(t, 1), :], ps[0:NP, 2:3, :]).then_inc(A_hi_set, 1)
                wait(act, U_done, t + 1)
                wait(act, U_stored, 16 * t)
                a.copy(U_sb, ps[:, 3, 0:KH * NP]).then_inc(U_set, 1)
                wait(act, U_set, t + 1)
                act.dma_start(U_dram[ds(t, 1), :, :].rearrange("t p n -> p (t n)"), U_sb).then_inc(U_stored, 16)

            build(0, 0, 0)
            build(1, 1, 0)
            over_blocks(act, step)
            act.wait_ge(xh_set, 2 * NT)
            act.dma_start(xh_dram.rearrange("t p d -> p t d"), x_all).then_inc(xh_stored, 16)
            act.wait_ge(m2T_done, 1)
            for k in range(KD):
                last = a.copy(m2T[:, k, :], ps[:, 4 + k, :])
            last.then_inc(m2T_set, 1)
            for c in range(KH):
                act.wait_ge(upd_done, c + 1)
                last = a.copy(w_upd[:, c, :], ps[:, c, :])
            a.copy(q_upd[:, :], ps[:, 6, 0:KH]).then_inc(upd_set, 1)

            def to_bf16(j, b):
                wait(act, sel_set, j + 1)
                wait(act, transposed, j - 1)
                a.copy(selb[:, b, :, :], sel[:, to_bf16.slot, :, :].bitcast(f32)).then_inc(selb_set, 1)
                to_bf16.slot = (to_bf16.slot + 1) % RING

            def evacuate(j, b):
                wait(act, transposed, j + 1)
                wait(act, z_done, 2 * (j - 1))
                a.copy(selT[:, b, :, :], tr_ps[b][:, 0:2, :])
                a.copy(eT[:, b, :, :], tr_ps[b][:, 2:4, :]).then_inc(lhs_set, 1)

            def pair(j, s, n):
                if not is_last(j, NPAIR - 1):
                    evacuate(j + 1, (s + 1) % 2)
                wait(act, z_summed, 2 * j + 1)
                wait(act, pair_done, j - 1)
                a.activation(hid[:, s % 2, :], g[:, s, 0, :], ACT.Relu).then_inc(hid_set, 1)
                if not is_last(j, NPAIR - 2):
                    to_bf16(j + 2, s % 2)
                wait(act, z_summed, 2 * j + 2)
                a.activation(hid_hi[:, s % 2, :], g[:, s, 1, :], ACT.Relu).then_inc(hid_set, 1)

            to_bf16.slot = 0
            to_bf16(0, 0)
            to_bf16(1, 1)
            evacuate(0, 0)
            over_pairs(act, pair)

            def evacuate_sums(t):
                wait(act, ST_done, t + 1)
                wait(act, u_done, t)
                a.copy(ST[:, :, 0:NP], ps[:, 0, :].rearrange("p (c n) -> p c n", n=128)[:, :, 0:NP]).then_inc(ST_set, 1)

            def store(t):
                wait(act, o_set, t + 1)
                act.dma_start(out.rearrange("(t p) d -> p t d", p=NP)[:, ds(t, 1), :],
                              o_sb.rearrange("p (t d) -> p t d", t=1)).then_inc(o_stored, 16)

            def finish(t, r, n):
                if not is_last(t, NT - 1):
                    evacuate_sums(t + 1)
                wait(act, u_summed, t + 1)
                a.activation(U_t[:, r, :], U_t[:, r, :], ACT.Relu).then_inc(u_set, 1)
                if not (isinstance(t, int) and t == 0):
                    store(t - 1)

            evacuate_sums(0)
            over_blocks(act, finish)
            store(NT - 1)
            act.wait_ge(o_stored, 16 * NT)

        @block.vector
        def _(dve):
            v = nc.vector
            steps = [0]

            def link(ins):
                steps[0] += 1
                ins.then_inc(chain, 1)
                dve.wait_ge(chain, steps[0])

            dve.wait_ge(iota_set, 3)
            dve.wait_ge(ids_loaded, 32)
            link(v.tensor_copy(local1, src_i))
            link(v.tensor_scalar(bucket, local1, 1.0 / NP, -(NP // 2) / NP, ALU.mult, ALU.add))
            link(v.tensor_scalar_add(bucket, bucket, ROUND))
            link(v.tensor_scalar_add(bucket, bucket, -ROUND))
            cols0, cum, cnt, pairs, ends, base = (small[:, k, :] for k in range(6))
            link(v.tensor_scalar_add(cols0, iota1[0:NP, 0:NT], -1.0))
            link(v.tensor_tensor(hot, bucket.rearrange("p (o c) -> p o c", o=1).to_broadcast([NP, NT, EC]),
                                 cols0.rearrange("p (a o) -> p a o", o=1).to_broadcast([NP, NT, EC]), ALU.is_equal))
            v.tensor_scalar(before, iota1[0:NP, 0:NP], part1[0:NP, :], None, ALU.is_gt)
            v.memset(epsc[:, :], EPS)
            v.memset(ones[:, :], 1.0)
            link(v.tensor_tensor_scan(run_f, hot_f, hot_f, 0.0, ALU.add, ALU.max))
            link(v.tensor_copy(cum, run[:, :, EC - 1:EC].rearrange("p a o -> p (a o)")))
            link(v.tensor_copy(cnt[:, 0:1], cum[:, 0:1]))
            v.tensor_tensor(cnt[:, 1:NT], cum[:, 1:NT], cum[:, 0:NT - 1], ALU.subtract).then_inc(counts_set, 1)
            for m in (ident, identb):
                v.tensor_scalar(m[:, :], iota1[:, :], part1[:, :], None, ALU.is_equal)
            link(v.tensor_scalar_add(local1, local1, 1.0))
            v.scalar_tensor_tensor(local1, bucket, -float(NP), local1, ALU.mult, ALU.add).then_inc(const_set, 1)
            dve.wait_ge(counts_summed, 1)
            tot_ps, bef_ps = ps[0:NP, 0, 0:NT], ps[0:NP, 1, 0:NT]
            link(v.tensor_scalar_add(small_i, tot_ps, float(PAIR - 1)))
            link(v.tensor_scalar(small_i, small_i, 8, None, ALU.logical_shift_right))
            link(v.tensor_copy(pairs, small_i))
            link(v.tensor_tensor_scan(ends, pairs, pairs, 0.0, ALU.add, ALU.max))
            link(v.tensor_tensor(base, ends, pairs, ALU.subtract))
            link(v.scalar_tensor_tensor(base, base, float(PAIR), bef_ps, ALU.mult, ALU.add))
            link(v.tensor_scalar_add(base, base, -1.0))
            link(v.tensor_tensor(base[:, 1:NT], base[:, 1:NT], cum[:, 0:NT - 1], ALU.subtract))

            def places(c0, c1):
                c, w = slice(c0, c1), c1 - c0
                link(v.tensor_tensor(run[:, :, c], run[:, :, c],
                                     base.rearrange("p (a o) -> p a o", o=1).to_broadcast([NP, NT, w]), ALU.add))
                link(v.tensor_tensor(run[:, :, c], run[:, :, c], hot[:, :, c], ALU.mult))
                link(v.tensor_reduce(place_f[:, c], run[:, :, c].rearrange("p a c -> p c a"), AX.X, ALU.add))
                link(v.tensor_copy(src_i[:, c], place_f[:, c]))
                link(v.tensor_scalar(place[:, c], src_i[:, c], 127, None, ALU.bitwise_and))
                link(v.tensor_scalar(src_i[:, c], src_i[:, c], 7, None, ALU.logical_shift_right))
                link(v.scalar_tensor_tensor(place[:, c], place[:, c], float(NTILE), src_i[:, c], ALU.mult, ALU.add))

            places(0, FIRST * BC)

            def ended_buckets():
                link(v.tensor_tensor(ends_diag, ends[0:NT, :], ident[0:NT, 0:NT], ALU.mult))
                link(v.tensor_reduce(ends_diag[:, 0:1], ends_diag, AX.X, ALU.add))
                v.tensor_scalar(ended, pair_iota, ends_diag[:, 0:1], None, ALU.is_ge).then_inc(ended_set, 1)

            def split_edge_weights():
                dve.wait_ge(we_loaded, 16)
                link(v.tensor_copy(we[1], we[0]))
                link(v.tensor_tensor(we[0], we[0], we[1], ALU.subtract))
                link(v.tensor_copy(we[2], we[0]))
                v.tensor_tensor(we[3], we[0], we[2], ALU.subtract).then_inc(we_split, 1)

            def build(t, r, n):
                slots = recb_bf[:, r, :, 4:].rearrange("p c (k d) -> p c k d", d=DE)
                e = ea[:, r, :, :]
                wait(dve, scattered[r], 16 * BC * n)
                cols = ds(BC * t, BC)
                v.tensor_copy(recb_i[:, r, :, 0], dst_i[:, cols])
                v.tensor_copy(recb[:, r, :, 1], local1[:, cols])
                v.tensor_copy(row_i[:, r, :], place[:, cols])
                wait(dve, e1_set, t + 1)
                v.tensor_tensor(e, e, slots[:, :, 0, :], ALU.subtract).then_inc(r1_set, 1)
                wait(dve, e2_set, t + 1)
                v.tensor_tensor(
                    slots[:, :, 6:8, :], e.rearrange("p c (o d) -> p c o d", o=1).to_broadcast([NP, BC, 2, DE]),
                    slots[:, :, 3:4, :].to_broadcast([NP, BC, 2, DE]), ALU.subtract).then_inc(rec_built, 1)

            def low_A(t):
                wait(dve, A_hi_set, t + 1)
                v.tensor_tensor(A_lo[:, ds(t, 1), :], ps[0:NP, 2:3, :], A_hi[:, ds(t, 1), :].bitcast(f32),
                                ALU.subtract).then_inc(A_lo_set, 1)

            def step(t, r, n):
                next_build(build, t, r, n)
                if isinstance(t, int) and t == 0:
                    split_edge_weights()
                else:
                    low_A(t - 1)
                cols = ds(BC * t, BC)
                if isinstance(t, int) and t == 0:
                    dve.wait_ge(x_loaded, 16)
                    dve.wait_ge(ub2_done, 1)
                    dve.wait_ge(buckets_counted, 1)
                    link(v.tensor_copy(ub2_rows, ps[0:NP, 7, 0:D]))
                    v.tensor_copy(pair_bucket[:, :], ps[0:1, 6, 0:NPAIR]).then_inc(order_done, 1)
                xt = x_all[:, ds(t, 1), :].rearrange("p t d -> p (t d)")
                v.bn_stats(stat[:, 0:6], xt).then_inc(norm_step, 1)
                wait(dve, norm_step, 3 * t + 1)
                dve.nop(nofuse=True)
                v.bn_aggr(stat[:, 6:8], stat[:, 0:6]).then_inc(norm_step, 1)
                wait(dve, std_set, t + 1)
                v.reciprocal(stat[:, 9:10], stat[:, 8:9]).then_inc(norm_step, 1)
                wait(dve, norm_step, 3 * t + 3)
                wait(dve, hT_done, t)
                v.tensor_scalar(h_t, xt, stat[:, 6:7], stat[:, 9:10], ALU.subtract, ALU.mult).then_inc(h_set, 1)
                wait(dve, h_set, 2 * t + 1)
                v.tensor_scalar_max(h_t, h_t, 0.0).then_inc(h_set, 1)
                wait(dve, h_set, 2 * t + 2)
                v.tensor_tensor(xt, xt, h_t, ALU.add).then_inc(xh_set, 1)
                wait(dve, xh_set, 2 * t + 1)
                v.tensor_tensor(xt, xt, ub2_rows, ALU.add).then_inc(xh_set, 1)
                wait(dve, hot_used, t)
                v.tensor_tensor(hot_b, bucket[:, cols].rearrange("p (c o) -> p c o", o=1).to_broadcast([NP, BC, NT]),
                                cols0.rearrange("p (o a) -> p o a", o=1).to_broadcast([NP, BC, NT]), ALU.is_equal)
                v.tensor_tensor(hot_n, local1[:, cols].rearrange("p (c o) -> p c o", o=1).to_broadcast([NP, BC, NP]),
                                iota1[0:NP, 0:NP].rearrange("p (o n) -> p o n", o=1).to_broadcast([NP, BC, NP]),
                                ALU.is_equal).then_inc(hot_set, 1)

            build(0, 0, 0)
            build(1, 1, 0)
            ended_buckets()
            places(FIRST * BC, EC)
            over_blocks(dve, step)
            low_A(NT - 1)

            dve.wait_ge(hot_used, NT)
            v.tensor_copy(cnt_sb, ps[0:NP, 5, 0:NT]).then_inc(cnt_set, 1)
            dve.wait_ge(cntT_done, 1)
            v.tensor_copy(cntT_sb, ps[0:NT, 4, 0:NP]).then_inc(cntT_set, 1)
            dve.wait_ge(xh_stored, 16)
            dve.wait_ge(cnt_stored, 16)
            dve.wait_ge(U_done, NT)
            dve.wait_ge(order_done, 1)
            dve.wait_ge(we_placed, 16 * NSLOT)
            v.memset(S_flat, 0.0).then_inc(S_zeroed, 1)
            dve.wait_ge(S_zeroed, 1)
            dve.wait_ge(upd_set, 1)

            def one_hots(j, s, n):
                wait(dve, rec_loaded[s], 16 * n + 16)
                wait(dve, pair_done, j - RING + 1)
                v.tensor_tensor(sel[:, s, :, :], iota1[:, :].rearrange("p (o n) -> p o n", o=1).to_broadcast([128, 2, 128]),
                                rec_f[:, s, :, 1:2].to_broadcast([128, 2, 128]), ALU.is_equal).then_inc(sel_set, 1)

            def add_sums(j, s):
                k = v.value_load(pair_bucket[0:1, ds(j, 1)], min_val=0, max_val=NT - 1)
                row = S[0:NP, ds(k, 1), :].rearrange("p t w -> p (t w)")
                wait(dve, pair_done, j + 1)
                wait(dve, S_added, j)
                v.tensor_tensor(row, row, S_ps[s % 2], ALU.add).then_inc(S_added, 1)

            def pair(j, s, n):
                for u in range(2):
                    wait(dve, gathered[s][u], 16 * n + 16)
                    wait(dve, z_done, 2 * j + u + 1)
                    v.tensor_tensor(g[:, s, u, :], z_ps[:, u, :], g[:, s, u, :], ALU.add).then_inc(z_summed, 1)
                if not (isinstance(j, int) and j == 0):
                    add_sums(j - 1, (s - 1) % RING)
                if not is_last(j, NPAIR - AHEAD):
                    one_hots(j + AHEAD, (s + AHEAD) % RING, n + (s + AHEAD) // RING)
                wait(dve, hid_set, 2 * j + 2)
                v.scalar_tensor_tensor(hid_lo[:, s % 2, :], g[:, s, 1, :], 0.0, hid_hi[:, s % 2, :].bitcast(f32),
                                       ALU.max, ALU.subtract).then_inc(lo_set, 1)

            for j in range(AHEAD):
                one_hots(j, j, 0)
            over_pairs(dve, pair)
            add_sums(NPAIR - 1, RING - 1)

            dve.wait_ge(S_added, NPAIR)
            dve.wait_ge(hid_set, 2 * NPAIR)
            dve.wait_ge(lo_set, NPAIR)

            def stage(t):
                wait(dve, ST_done, t)
                v.tensor_copy(S_t, S[0:NP, ds(t, 1), :].rearrange("p t w -> p (t w)")).then_inc(S_t_set, 1)

            def output(t):
                wait(dve, o_done, t + 1)
                wait(dve, o_stored, 16 * t)
                v.tensor_tensor(o_sb, ps[0:NP, 4, 0:D], xh_all[:, ds(t, 1), :].rearrange("p t d -> p (t d)"),
                                ALU.add).then_inc(o_set, 1)

            def finish(t, r, n):
                if not is_last(t, NT - 1):
                    stage(t + 1)
                wait(dve, U_loaded[r], 16 * n + 16)
                for c in range(KH):
                    U = U_t[:, r, c * NP:(c + 1) * NP]
                    last = v.scalar_tensor_tensor(U, cnt_rows[:, ds(NP * t, NP)], q_upd[:, c:c + 1], U,
                                                  ALU.mult, ALU.add)
                last.then_inc(node_step, 1)
                wait(dve, node_step, t + 1)
                wait(dve, u_done, t + 1)
                v.tensor_tensor(U_t[:, r, :], ps[:, 3, 0:KH * NP], U_t[:, r, :], ALU.add).then_inc(u_summed, 1)
                if not (isinstance(t, int) and t == 0):
                    output(t - 1)

            stage(0)
            dve.wait_ge(xh_loaded, 32)
            over_blocks(dve, finish)
            output(NT - 1)

        @block.tensor
        def _(pe):
            mm = nc.tensor.matmul
            pe.wait_ge(counts_set, 1)
            cnt = small[:, 2, :]
            mm(ps[0:NP, 0, 0:NT], ones[0:NP, 0:NP], cnt, start=True, stop=True)
            mm(ps[0:NP, 1, 0:NT], before, cnt, start=True, stop=True).then_inc(counts_summed, 1)
            pe.wait_ge(const_set, 1)
            pe.wait_ge(w_loaded, 16 * (6 + KD))
            mm(ps[0:NP, 7, 0:D], ones[0:1, 0:NP], bias_out, start=True, stop=True).then_inc(ub2_done, 1)
            pe.wait_ge(ended_set, 1)
            mm(ps[0:1, 6, 0:NPAIR], ones[0:NT - 1, 0:1], ended[0:NT - 1, :], start=True, stop=True
               ).then_inc(buckets_counted, 1)

            def step(t, r, n):
                wait(pe, h_set, 2 * t + 2)
                wait(pe, hT_set, t)
                for k in range(KD):
                    last = nc.tensor.transpose(ps[:, 0, k * 128:k * 128 + NP], h_t[:, k * 128:(k + 1) * 128],
                                               ident[0:NP, 0:NP])
                last.then_inc(hT_done, 1)
                wait(pe, hT_set, t + 1)
                wait(pe, B_set, t)
                for k in range(KD):
                    last = mm(ps[0:NP, 1, :], hT[:, k, 0:NP], w_dst[:, k, :], start=k == 0, stop=k == KD - 1)
                last.then_inc(B_done, 1)
                wait(pe, A_lo_set, t)
                for k in range(KD):
                    mm(ps[0:NP, 2, :], hT[:, k, 0:NP], w_src[:, k, :], start=k == 0, stop=False)
                mm(ps[0:NP, 2, :], ones[0:1, 0:NP], bias1[:, 0:H], start=False, stop=True).then_inc(A_done, 1)
                wait(pe, U_set, t)
                for c in range(KH):
                    o = ps[:, 3, c * NP:(c + 1) * NP]
                    for k in range(KD):
                        mm(o, w_node[:, k, c * 128:(c + 1) * 128], hT[:, k, 0:NP], start=k == 0, stop=False)
                    last = mm(o, bias1[:, H + c * 128:H + (c + 1) * 128], ones[0:1, 0:NP], start=False, stop=True)
                last.then_inc(U_done, 1)
                wait(pe, hot_set, t + 1)
                for k in range(BC):
                    first = isinstance(t, int) and t == 0 and k == 0
                    end = is_last(t, NT - 1) and k == BC - 1
                    last = mm(ps[0:NP, 5, 0:NT], hot_n[:, k, :], hot_b[:, k, :], start=first, stop=end,
                              skip_group_check=True)
                last.then_inc(hot_used, 1)

            over_blocks(pe, step)
            pe.wait_ge(we_placed, 16 * NSLOT)
            pe.wait_ge(order_done, 1)
            pe.wait_ge(cnt_set, 1)
            nc.tensor.transpose(ps[0:NT, 4, 0:NP], cnt_sb, ident[0:NP, 0:NP]).then_inc(cntT_done, 1)
            pe.wait_ge(w3_loaded, 48)
            pe.wait_ge(B_set, NT)
            pe.wait_ge(A_lo_set, NT)
            pe.wait_ge(U_set, NT)
            pe.wait_ge(cntT_set, 1)
            for k in range(KD):
                for c in range(KH):
                    last = nc.tensor.transpose(ps[:, 4 + k, c * 128:(c + 1) * 128],
                                               w_msg2[:, c, k * 128:(k + 1) * 128], ident[:, :])
            last.then_inc(m2T_done, 1)
            for c in range(KH):
                for k in range(KD):
                    mm(ps[:, 6, c:c + 1], w_agg[:, k, c * 128:(c + 1) * 128], mb2_cols[:, k:k + 1],
                       start=k == 0, stop=k == KD - 1)
            pe.wait_ge(m2T_set, 1)
            for c in range(KH):
                for k in range(KD):
                    last = mm(ps[:, c, :], m2T[:, k, c * 128:(c + 1) * 128], w_agg[:, k, :],
                              start=k == 0, stop=k == KD - 1)
                last.then_inc(upd_done, 1)
            pe.wait_ge(upd_set, 1)

            def transposes(j, s):
                wait(pe, selb_set, j + 1)
                wait(pe, lhs_set, j - 1)
                for u in range(2):
                    nc.tensor.transpose(tr_ps[s % 2][:, u, :], selb[:, s % 2, u, :], identb[:, :])
                    last = nc.tensor.transpose(tr_ps[s % 2][:, 2 + u, :], rec_bf[:, s, u, 4:], identb[:, :])
                last.then_inc(transposed, 1)

            def pre_relu(j, s, u, k):
                wait(pe, lhs_set, j + 1)
                wait(pe, z_summed, 2 * (j - 1) + u + 1)
                b = s % 2
                for n, part in enumerate((A_hi, A_lo)):
                    mm(z_ps[:, u, :], selT[0:NP, b, u, :], part[:, ds(k, 1), :].rearrange("p t h -> p (t h)"),
                       start=n == 0, stop=False)
                mm(z_ps[:, u, :], eT[:, b, u, :], w_edge[:, :], start=False, stop=True).then_inc(z_done, 1)

            def sums(j, s, u):
                wait(pe, hid_set, 2 * j + u + 1)
                b = s % 2
                if u == 0:
                    wait(pe, S_added, j - 1)
                    mm(S_ps[b], sel[:, s, 0, 0:NP].bitcast(f32), hid[:, b, :], start=True, stop=False)
                else:
                    wait(pe, lo_set, j + 1)
                    mm(S_ps[b], sel[:, s, 1, 0:NP], hid_hi[:, b, :], start=False, stop=False)
                    mm(S_ps[b], sel[:, s, 1, 0:NP], hid_lo[:, b, :], start=False, stop=True).then_inc(pair_done, 1)

            def pair(j, s, n):
                first = isinstance(j, int) and j == 0
                k = nc.tensor.value_load(pair_bucket[0:1, ds(j, 1)], min_val=0, max_val=NT - 1)
                pre_relu(j, s, 0, k)
                if not is_last(j, NPAIR - 1):
                    transposes(j + 1, (s + 1) % RING)
                if not first:
                    sums(j - 1, (s - 1) % RING, 0)
                pre_relu(j, s, 1, k)
                if not first:
                    sums(j - 1, (s - 1) % RING, 1)

            transposes(0, 0)
            over_pairs(pe, pair)
            sums(NPAIR - 1, RING - 1, 0)
            sums(NPAIR - 1, RING - 1, 1)

            def transpose_sums(t):
                wait(pe, S_t_set, t + 1)
                wait(pe, ST_set, t)
                for c in range(KH):
                    last = nc.tensor.transpose(ps[:, 0, c * 128:c * 128 + NP], S_t[:, c * 128:(c + 1) * 128],
                                               ident[0:NP, 0:NP])
                last.then_inc(ST_done, 1)

            def output(t, r):
                wait(pe, u_set, t + 1)
                wait(pe, o_set, t)
                for c in range(KH):
                    last = mm(ps[0:NP, 4, 0:D], U_t[:, r, c * NP:(c + 1) * NP], w_out[:, c, :],
                              start=c == 0, stop=c == KH - 1)
                last.then_inc(o_done, 1)

            def finish(t, r, n):
                wait(pe, ST_set, t + 1)
                wait(pe, u_summed, t)
                for c in range(KH):
                    for k in range(KH):
                        last = mm(ps[:, 3, c * NP:(c + 1) * NP], w_upd[:, k, c * 128:(c + 1) * 128], ST[:, k, 0:NP],
                                  start=k == 0, stop=k == KH - 1)
                last.then_inc(u_done, 1)
                if not is_last(t, NT - 1):
                    transpose_sums(t + 1)
                if not (isinstance(t, int) and t == 0):
                    output(t - 1, 1 - r)

            transpose_sums(0)
            over_blocks(pe, finish)
            output(NT - 1, (NT - 1) % 2)


_INS = ['x', 'src', 'dst', 'edge_attr_16', 'L0_gnn_mW1', 'L0_gnn_mb1', 'L0_gnn_mW2', 'L0_gnn_mb2', 'L0_gnn_uW1',
        'L0_gnn_ub1', 'L0_gnn_uW2', 'L0_gnn_ub2']


def kernel(**inputs):
    import numpy as _np
    import concourse.bacc as _bacc
    from concourse import mybir as _mybir
    from concourse.bass_utils import run_bass_kernel_spmd as _run

    nc = _bacc.Bacc("TRN2", target_bir_lowering=False, num_devices=1)
    arrays, args = {}, []
    for name in _INS:
        a = _np.ascontiguousarray(inputs[name])
        arrays[f"in_{name}_dram"] = a
        args.append(nc.dram_tensor(f"in_{name}_dram", a.shape, _mybir.dt.from_np(a.dtype), kind="ExternalInput").ap())
    shape = inputs['x'].shape
    args.append(nc.dram_tensor("out_dram", shape, _mybir.dt.float32, kind="ExternalOutput").ap())
    gnn_layer_kernel(nc, *args)
    r = _run(nc, [arrays], core_ids=[0])
    return r.results[0]["out_dram"]
```

```python
import concourse.bass as bass
import numpy as np
from concourse import mybir
from contextlib import ExitStack


def gnn_layer_kernel(nc, x, src, dst, edge_attr, mW1, mb1, mW2, mb2, uW1, ub1, uW2, ub2, out):
    f32, f32r, bf16, i32 = mybir.dt.float32, mybir.dt.float32r, mybir.dt.bfloat16, mybir.dt.int32
    ALU = mybir.AluOpType
    ACT = mybir.ActivationFunctionType
    AX = mybir.AxisListType
    ds = bass.ds

    N, D = x.shape
    E, DE = edge_attr.shape
    H = mW1.shape[1]
    NP = 125
    NT = N // NP
    EC = E // NP
    KD = D // 128
    KH = H // 128
    PAIR = 256
    RING = 4
    UNROLL = 16
    NPAIR = (E + NT * (PAIR - 1)) // PAIR
    NPAIR += -(NPAIR - 2 * RING) % UNROLL
    MIN_PAIRS = -(-E // PAIR)
    NTILE = 2 * (NPAIR + NT)
    BC = EC // NT
    NSLOT = 8
    REC = 2 + NSLOT * DE // 2
    AHEAD = 3
    FIRST = 2
    EPS = 1e-5
    ROUND = 12582912.0
    assert NP * NT == N and NP * EC == E and BC * NT == EC and NT % 2 == 1

    records = nc.dram_tensor("records", (128 * NTILE, REC), f32).ap()
    B_dram = nc.dram_tensor("B_dram", (N, H), f32).ap()
    cnt_dram = nc.dram_tensor("cnt_dram", (NT, NP), f32).ap()
    U_dram = nc.dram_tensor("U_dram", (NT, 128, KH * NP), f32).ap()
    xh_dram = nc.dram_tensor("xh_dram", (NT, NP, D), f32).ap()
    upd_dram = nc.dram_tensor("upd_dram", (KH, 128, H), f32).ap()

    ctx = ExitStack()
    with ctx:
        def sb(name, shape, dt=f32):
            return ctx.enter_context(nc.sbuf_tensor(name, shape, dt))

        def sem(name):
            return ctx.enter_context(nc.semaphore(name))

        def carver(flat):
            used = [0]

            def carve(rows, words):
                used[0] += words
                assert used[0] <= flat.shape[1]
                return flat[0:rows, used[0] - words:used[0]]
            return carve

        w_in = sb("w_in", [128, KH, H])
        w_src, w_dst = w_in[:, 0:KD, :], w_in[:, KD:KH, :]
        w_upd = w_in
        w_node = sb("w_node", [128, KD, H])
        w_out = w_node[:, :, :].rearrange("p k (a d) -> p (k a) d", d=D)
        w_edge = sb("w_edge", [128, H], bf16)
        q_upd = sb("q_upd", [128, KH])
        mb2_cols = sb("mb2_cols", [128, KD])
        iota1 = sb("iota1", [128, 128])
        iotab = sb("iotab", [128, 128], bf16)
        part1 = sb("part1", [128, 1])
        ident = sb("ident", [128, 128])
        identb = sb("identb", [128, 128], bf16)
        ones = sb("ones", [128, 128])
        epsc = sb("epsc", [128, 1])
        pair_bucket = sb("pair_bucket", [1, NPAIR], i32)
        last_pair = sb("last_pair", [1, NT], i32)

        S = sb("S", [128, NT, H])
        S_flat = S[:, :, :].rearrange("p t w -> p (t w)")
        carve = carver(S_flat)
        x_all = carve(NP, NT * D).rearrange("p (t d) -> p t d", d=D)
        cnt_sb = carve(NP, NT)
        cntT_sb = carve(NT, NP)
        zero_from = NT * D + NT + NP
        src_i = carve(NP, EC).bitcast(i32)
        dst_i = carve(NP, EC).bitcast(i32)
        place = carve(NP, EC).bitcast(i32)
        place_f = carve(NP, EC)
        local1 = carve(NP, EC)
        bucket = carve(NP, EC)
        small = carve(NP, 6 * NT).rearrange("p (k a) -> p k a", a=NT)
        small_i = carve(NP, NT).bitcast(i32)
        pair_iota = carve(NT, NPAIR)
        ended = carve(NT, NPAIR)
        ends_diag = carve(NT, NT)
        to_spare = carve(1, NT)
        bias1 = carve(1, 2 * H)
        bias_out = carve(1, D)
        ub2_rows = carve(NP, D)
        before = carve(NP, NP)
        we = [carve(DE, H)] + [carve(DE, H // 2).bitcast(bf16) for _ in range(3)]

        mid = sb("mid", [128, RING * 2 * H])
        g = mid[:, :].rearrange("p (r u h) -> p r u h", r=RING, u=2)
        carve = carver(mid[:, :])
        zero = carve(128, 8 * REC)
        recb_f = carve(NP, 2 * BC * REC)
        recb = recb_f.rearrange("p (r c w) -> p r c w", r=2, c=BC)
        recb_i = recb_f.bitcast(i32).rearrange("p (r c w) -> p r c w", r=2, c=BC)
        recb_bf = recb_f.bitcast(bf16).rearrange("p (r c w) -> p r c w", r=2, c=BC)
        row_i = carve(NP, 2 * BC).bitcast(i32).rearrange("p (r c) -> p r c", r=2)
        upd_sb = [carve(128, H)]
        ea = carve(NP, 2 * BC * DE).rearrange("p (r c d) -> p r c d", r=2, c=BC)
        carve = carver(mid[:, :])
        S_t = carve(NP, H)
        ST = carve(128, KH * 128).rearrange("p (c n) -> p c n", n=128)
        o_sb = carve(NP, D)
        U_t = carve(128, 2 * KH * NP).rearrange("p (b n) -> p b n", b=2)

        rec = sb("rec", [128, RING * 2 * REC])
        rec_i = rec[:, :].bitcast(i32).rearrange("p (r u w) -> p r u w", r=RING, u=2)
        rec_bf = rec[:, :].bitcast(bf16).rearrange("p (r u w) -> p r u w", r=RING, u=2)
        hot_b = rec[0:NP, 0:(BC * NT + 1) // 2].bitcast(bf16)[:, 0:BC * NT].rearrange("p (c a) -> p c a", a=NT)
        selb = sb("selb", [128, RING, 2, 128], bf16)
        upd_sb.append(selb[:, :, :, :].rearrange("p r u n -> p (r u n)").bitcast(f32))
        eT = sb("eT", [128, 2, 2, 128], bf16)
        hid = sb("hid", [128, 2, H])
        hT = hid[:, 0, 0:KD * 128].rearrange("p (k n) -> p k n", n=128)
        stat = hid[0:NP, 0, KD * 128:KD * 128 + 16]
        h_t = hid[0:NP, 1, 0:D]

        def sharing(name, *sets):
            for tensors in sets:
                with ExitStack() as one:
                    yield [one.enter_context(nc.sbuf_tensor(*t)) for t in tensors]
            sb(name, [128, max(sum(int(np.prod(shape[1:])) for _, shape, _ in tensors) for tensors in sets)])

        (run_t, hot_t), (A_hi, A_lo), (late,) = sharing(
            "kept1", (("run_t", [NP, NT * EC], f32), ("hot_t", [NP, NT * EC], f32)),
            (("A_hi", [NP, NT, H], f32r), ("A_lo", [NP, NT, H], f32r)),
            (("late", [128, 2 * NT * H], f32),))
        run_f, hot_f = run_t[:, :], hot_t[:, :]
        run = run_f.rearrange("p (a c) -> p a c", c=EC)
        hot = hot_f.rearrange("p (a c) -> p a c", c=EC)
        carve = carver(late[:, :])
        U_all = carve(128, NT * KH * NP)
        xh_all = carve(NP, NT * D)
        cnt_rows = carve(128, N)
        (tiles,), (sel, selT, hid_hi, hid_lo) = sharing(
            "kept2", (("tiles", [128, (4 + KD) * H], f32),),
            (("sel", [128, 2, 2, 128], f32r), ("selT", [128, 2, 2, 128], f32r),
             ("hid_hi", [128, 2, H], f32r), ("hid_lo", [128, 2, H], f32r)))
        B_sb = tiles[0:NP, 0:H]
        U_sb = tiles[:, H:H + KH * NP]
        hot_n = tiles[0:NP, 2 * H:2 * H + (BC * NP + 1) // 2].bitcast(bf16)[:, 0:BC * NP].rearrange(
            "p (c n) -> p c n", n=NP)
        w_agg = tiles[:, 0:KD * H].rearrange("p (k h) -> p k h", k=KD)
        w_msg2 = tiles[:, KD * H:4 * H].rearrange("p (k d) -> p k d", d=D)
        m2T = tiles[:, 4 * H:].rearrange("p (k h) -> p k h", k=KD)

        ps = ctx.enter_context(nc.psum_tensor("ps", [128, 8, 512], f32))
        z_ps = ps[:, 0:2, :]
        S_ps = [ps[0:NP, 2 + b, :] for b in range(2)]
        tr_ps = [ps[:, 6 + b, :].bitcast(bf16).rearrange("p (k n) -> p k n", n=128) for b in range(2)]

        ids_loaded, x_loaded, w_loaded, we_loaded = sem("ids_loaded"), sem("x_loaded"), sem("w_loaded"), sem("we_loaded")
        we_split, we_placed, w3_loaded = sem("we_split"), sem("we_placed"), sem("w3_loaded")
        ea_loaded = [sem(f"ea_loaded{r}") for r in range(2)]
        zero_set, iota_set, const_set = sem("zero_set"), sem("iota_set"), sem("const_set")
        zeroed = [sem(f"zeroed{share}") for share in range(3)]
        tail_zeroed, last_pair_set = sem("tail_zeroed"), sem("last_pair_set")
        chain = sem("chain")
        counts_set, counts_summed, order_done = sem("counts_set"), sem("counts_summed"), sem("order_done")
        order_started, ended_set, buckets_counted = sem("order_started"), sem("ended_set"), sem("buckets_counted")
        hot_set, hot_used, cnt_stored = sem("hot_set"), sem("hot_used"), sem("cnt_stored")
        e1_set, r1_set, e2_set, rec_built = sem("e1_set"), sem("r1_set"), sem("e2_set"), sem("rec_built")
        scattered = [sem(f"scattered{r}") for r in range(2)]
        norm_step, std_set, h_set, xh_set = sem("norm_step"), sem("std_set"), sem("h_set"), sem("xh_set")
        hT_done, B_done, A_done, U_done = sem("hT_done"), sem("B_done"), sem("A_done"), sem("U_done")
        hT_set, B_set, A_hi_set, A_lo_set, U_set = (sem("hT_set"), sem("B_set"), sem("A_hi_set"), sem("A_lo_set"),
                                                    sem("U_set"))
        B_stored, U_stored, S_zeroed = sem("B_stored"), sem("U_stored"), sem("S_zeroed")
        xh_stored = [sem(f"xh_stored{r}") for r in range(2)]
        rec_loaded = [sem(f"rec_loaded{r}") for r in range(RING)]
        gathered = [[sem(f"gathered{r}_{u}") for u in range(2)] for r in range(RING)]
        selb_set, transposed, lhs_set = sem("selb_set"), sem("transposed"), sem("lhs_set")
        lo_set = sem("lo_set")
        z_done, z_summed, hid_set, pair_done, S_added = (sem("z_done"), sem("z_summed"), sem("hid_set"),
                                                         sem("pair_done"), sem("S_added"))
        upd_loaded = sem("upd_loaded")
        late_loaded = [sem(f"late_loaded{b}") for b in range(2)]
        m2T_done, m2T_set, upd_done, upd_set = sem("m2T_done"), sem("m2T_set"), sem("upd_done"), sem("upd_set")
        cnt_set, cntT_done, cntT_set = sem("cnt_set"), sem("cntT_done"), sem("cntT_set")
        ub2_done, q_set = sem("ub2_done"), sem("q_set")
        upd_stored = [sem(f"upd_stored{b}") for b in range(2)]
        S_t_set, ST_done, ST_set, node_step = sem("S_t_set"), sem("ST_done"), sem("ST_set"), sem("node_step")
        u_done, u_summed, u_set = sem("u_done"), sem("u_summed"), sem("u_set")
        o_done, o_set, o_stored = sem("o_done"), sem("o_set"), sem("o_stored")

        nop_engines = []
        block = ctx.enter_context(nc.Block())

        def wait(eng, s, n):
            if isinstance(n, int):
                if n > 0:
                    eng.wait_ge(s, n)
            else:
                eng.wait_ge(s, n)
                if eng in nop_engines:
                    eng.nop(nofuse=True)

        def over_blocks(eng, step):
            for t in range(5):
                step(t, t % 2, t // 2)
            with eng.Fori(2, NT // 2 - 1) as i:
                step(2 * i + 1, 1, i)
                step(2 * i + 2, 0, i + 1)
            for t in range(NT - 2, NT):
                step(t, t % 2, t // 2)

        def next_build(build, t, r, n):
            if isinstance(t, int) and t < 3:
                build(t + 2, r, n + 1)
            elif not (isinstance(t, int) and t in (3, NT - 1)):
                build(t + 1, 1 - r, n + r)

        def over_pairs(eng, step):
            for j in range(RING):
                step(j, j, 0)
            with eng.Fori(0, (NPAIR - 2 * RING) // UNROLL) as i:
                for s in range(UNROLL):
                    step(UNROLL * i + RING + s, s % RING, UNROLL // RING * i + 1 + s // RING)
            for j in range(NPAIR - RING, NPAIR):
                step(j, j % RING, j // RING)

        def is_last(j, n):
            return isinstance(j, int) and j >= n

        rec_v = records.rearrange("(p c) w -> p (c w)", c=NTILE)
        SHARES = (0, (NT + 2) // 3, (NT + 3) // 2, NT)

        def zero_last_pairs(eng, share):
            eng.wait_ge(last_pair_set, 1)
            eng.wait_ge(tail_zeroed, 16)
            with eng.Fori(SHARES[share], SHARES[share + 1]) as a:
                k = eng.value_load(last_pair[0:1, ds(a, 1)], min_val=0, max_val=NPAIR + NT - 1)
                eng.dma_start(rec_v[:, ds(2 * REC * k, 2 * REC)], zero[:, 0:2 * REC]).then_inc(zeroed[share], 16)

        @block.sync
        def _(sp):
            nop_engines.append(sp)
            sp.dma_start(src_i, src.rearrange("(p c) -> p c", c=EC)).then_inc(ids_loaded, 16)
            sp.dma_start(dst_i, dst.rearrange("(p c) -> p c", c=EC)).then_inc(ids_loaded, 16)
            ea_v = edge_attr.rearrange("(p b c) d -> p b (c d)", b=NT, c=BC)
            for r in range(2):
                sp.dma_start(ea[:, r, :, :].rearrange("p c d -> p (c d)"), ea_v[:, r, :]).then_inc(ea_loaded[r], 16)
            sp.wait_ge(zero_set, 1)
            sp.dma_start(rec_v[:, 2 * REC * MIN_PAIRS:2 * REC * NPAIR].rearrange("p (b w) -> p b w", w=2 * REC),
                         zero[:, 0:2 * REC].rearrange("p (o w) -> p o w", o=1).to_broadcast(
                             [128, NPAIR - MIN_PAIRS, 2 * REC])).then_inc(tail_zeroed, 16)
            for w, m in ((w_agg, uW1[D:2 * D, :]), (w_msg2, mW2)):
                sp.dma_start(w, m.rearrange("(k p) h -> p k h", p=128)).then_inc(w3_loaded, 16)
            for k in range(KD):
                sp.dma_start(mb2_cols[:, k:k + 1], mb2[k * 128:(k + 1) * 128].rearrange("(p o) -> p o", o=1)
                             ).then_inc(w3_loaded, 16)
            for w, m in ((w_src, mW1[0:D, :]), (w_dst, mW1[D:2 * D, :]), (w_node[:, :, :], uW1[0:D, :])):
                sp.dma_start(w, m.rearrange("(k p) h -> p k h", p=128)).then_inc(w_loaded, 16)
            for row, b in ((bias1[:, 0:H], mb1), (bias1[:, H:2 * H], ub1), (bias_out, ub2)):
                sp.dma_start(row, b.rearrange("(o h) -> o h", o=1)).then_inc(w_loaded, 16)
            sp.dma_start(we[0], mW1[2 * D:2 * D + DE, :]).then_inc(we_loaded, 16)
            sp.dma_start(x_all, x.rearrange("(t p) d -> p t d", p=NP)).then_inc(x_loaded, 16)
            zero_last_pairs(sp, 0)

            def load_edges(t, r, n):
                if not (isinstance(t, int) and t < 2):
                    wait(sp, rec_built, t - 1)
                    sp.dma_start(ea[:, r, :, :].rearrange("p c d -> p (c d)"),
                                 ea_v[:, ds(t, 1), :].rearrange("p b w -> p (b w)")).then_inc(ea_loaded[r], 16)
                if isinstance(t, int) and t == 2:
                    sp.wait_ge(we_split, 1)
                    for k in range(NSLOT):
                        sp.dma_start(w_edge[k * DE:(k + 1) * DE, :], we[1 + k % 3]).then_inc(we_placed, 16)

            over_blocks(sp, load_edges)

            sp.wait_ge(U_done, NT)
            sp.wait_ge(hot_used, NT)
            sp.wait_ge(cntT_set, 1)
            sp.dma_start(cnt_dram[:, :], cntT_sb).then_inc(cnt_stored, 16)
            for r in range(2):
                sp.wait_ge(scattered[r], 16 * BC * (NT // 2 + 1 - r))

            def load_records(j, s, n):
                wait(sp, transposed, j - RING + 1)
                wait(sp, z_summed, 2 * (j - RING + 1))
                sp.dma_start(rec[:, s * 2 * REC:(s + 1) * 2 * REC],
                             rec_v[:, ds(2 * REC * j, 2 * REC)]).then_inc(rec_loaded[s], 16)

            over_pairs(sp, load_records)

            for b in range(2):
                sp.wait_ge(upd_stored[b], 16 * (KH // 2))
            sp.dma_start(w_upd[:, :, :], upd_dram.rearrange("k p h -> p k h")).then_inc(upd_loaded, 16)
            sp.dma_start(w_out, uW2.rearrange("(k p) h -> p k h", p=128)).then_inc(upd_loaded, 16)

            sp.wait_ge(z_done, 2 * NPAIR)
            for r in range(2):
                sp.wait_ge(xh_stored[r], 16 * (NT // 2 + 1 - r))
            sp.wait_ge(U_stored, 16 * NT)
            sp.wait_ge(cnt_stored, 16)

            def load_late(t, r, n):
                wait(sp, late_loaded[r], 48 * n)
                sp.dma_start(U_all[:, ds(KH * NP * t, KH * NP)], U_dram[ds(t, 1), :, :].rearrange("t p n -> p (t n)")
                             ).then_inc(late_loaded[r], 16)
                sp.dma_start(xh_all[:, ds(D * t, D)], xh_dram[ds(t, 1), :, :].rearrange("t p d -> p (t d)")
                             ).then_inc(late_loaded[r], 16)
                sp.dma_start(cnt_rows[:, ds(NP * t, NP)], cnt_dram[ds(t, 1), :].to_broadcast([128, NP])
                             ).then_inc(late_loaded[r], 16)

            over_blocks(sp, load_late)

        @block.gpsimd
        def _(pool):
            nop_engines.append(pool)
            nc.gpsimd.memset(zero, 0.0).then_inc(zero_set, 1)
            for out_ap, pattern, base, mult in ((iota1[:, :], [[1, 128]], 1, 0), (part1[:, :], [[0, 1]], 1, 1),
                                                (pair_iota, [[1, NPAIR]], 0, 0)):
                nc.gpsimd.iota(out_ap, pattern=pattern, base=base, channel_multiplier=mult,
                               allow_small_or_imprecise_dtypes=True).then_inc(iota_set, 1)
            zero_last_pairs(pool, 2)
            for share in range(3):
                pool.wait_ge(zeroed[share], 16 * (SHARES[share + 1] - SHARES[share]))

            def scatter(t, r, n):
                wait(pool, rec_built, t + 1)
                for k in range(BC):
                    nc.gpsimd.indirect_dma_start(
                        records[:, :], bass.IndirectOffsetOnAxis(ap=row_i[:, r, k:k + 1], axis=0),
                        recb[:, r, k, :], None).then_inc(scattered[r], 16)

            over_blocks(pool, scatter)
            for r in range(2):
                pool.wait_ge(scattered[r], 16 * BC * (NT // 2 + 1 - r))
            pool.wait_ge(B_stored, 16 * NT)

            def gather(j, s, n):
                wait(pool, rec_loaded[s], 16 * n + 16)
                for u in range(2):
                    wait(pool, hid_set, 2 * (j - RING) + u + 1)
                    if u == 1:
                        wait(pool, lo_set, j - RING + 1)
                    nc.gpsimd.indirect_dma_start(
                        g[:, s, u, :], None, B_dram[:, :],
                        bass.IndirectOffsetOnAxis(ap=rec_i[:, s, u, 0:1], axis=0)).then_inc(gathered[s][u], 16)

            over_pairs(pool, gather)

        @block.scalar
        def _(act):
            a = nc.scalar

            def build(t, r, n):
                slots = recb_bf[:, r, :, 4:].rearrange("p c (k d) -> p c k d", d=DE)
                e = ea[:, r, :, :].rearrange("p c (o d) -> p c o d", o=1).to_broadcast([NP, BC, 3, DE])
                wait(act, ea_loaded[r], 16 * n + 16)
                wait(act, scattered[r], 16 * BC * n)
                a.copy(slots[:, :, 0:3, :], e).then_inc(e1_set, 1)
                if isinstance(t, int) and t == 0:
                    zero_last_pairs(act, 1)
                wait(act, r1_set, t + 1)
                a.copy(slots[:, :, 3:6, :], e).then_inc(e2_set, 1)

            def rest(t, r):
                wait(act, A_done, t + 1)
                a.copy(A_hi[:, ds(t, 1), :], ps[0:NP, 2:3, :]).then_inc(A_hi_set, 1)
                wait(act, U_done, t + 1)
                wait(act, U_stored, 16 * t)
                a.copy(U_sb, ps[:, 3, 0:KH * NP]).then_inc(U_set, 1)
                wait(act, U_set, t + 1)
                act.dma_start(U_dram[ds(t, 1), :, :].rearrange("t p n -> p (t n)"), U_sb).then_inc(U_stored, 16)
                wait(act, xh_set, 2 * t + 2)
                act.dma_start(xh_dram[ds(t, 1), :, :].rearrange("t p d -> p (t d)"),
                              x_all[:, ds(t, 1), :].rearrange("p t d -> p (t d)")).then_inc(xh_stored[r], 16)

            def step(t, r, n):
                next_build(build, t, r, n)
                if not (isinstance(t, int) and t == 0):
                    rest(t - 1, 1 - r)
                wait(act, norm_step, 3 * t + 2)
                a.activation(stat[:, 8:9], stat[:, 7:8], ACT.Sqrt, bias=epsc[0:NP, :]).then_inc(std_set, 1)
                wait(act, hT_done, t + 1)
                wait(act, U_done, t)
                a.copy(hT[:, :, 0:NP], ps[:, 0, 0:KD * 128].rearrange("p (k n) -> p k n", n=128)[:, :, 0:NP]
                       ).then_inc(hT_set, 1)
                wait(act, B_done, t + 1)
                wait(act, B_stored, 16 * t)
                a.copy(B_sb, ps[0:NP, 1, :]).then_inc(B_set, 1)
                wait(act, B_set, t + 1)
                act.dma_start(B_dram.rearrange("(t p) h -> p t h", p=NP)[:, ds(t, 1), :],
                              B_sb.rearrange("p (t h) -> p t h", t=1)).then_inc(B_stored, 16)

            build(0, 0, 0)
            build(1, 1, 0)
            act.wait_ge(m2T_done, 1)
            for k in range(KD):
                last = a.copy(m2T[:, k, :], ps[:, 4 + k, :])
            last.then_inc(m2T_set, 1)
            for c in range(KH):
                act.wait_ge(upd_done, c + 1)
                if c >= 2:
                    act.wait_ge(upd_stored[c % 2], 16 * (c // 2))
                a.copy(upd_sb[c % 2], ps[:, c, :]).then_inc(upd_set, 1)
                act.wait_ge(upd_set, c + 1)
                act.dma_start(upd_dram[c, :, :], upd_sb[c % 2]).then_inc(upd_stored[c % 2], 16)
            a.copy(q_upd[:, :], ps[:, 6, 0:KH]).then_inc(q_set, 1)

            act.wait_ge(const_set, 1)
            over_blocks(act, step)
            rest(NT - 1, (NT - 1) % 2)

            def evacuate(j, b):
                wait(act, transposed, j + 1)
                wait(act, z_done, 2 * (j - 1))
                a.copy(selT[:, b, :, :], tr_ps[b][:, 0:2, :])
                a.copy(eT[:, b, :, :], tr_ps[b][:, 2:4, :]).then_inc(lhs_set, 1)

            def pair(j, s, n):
                if not is_last(j, NPAIR - 1):
                    evacuate(j + 1, (s + 1) % 2)
                wait(act, selb_set, j + 1)
                wait(act, pair_done, j - 1)
                a.copy(sel[:, s % 2, :, :], selb[:, s, :, :])
                wait(act, z_summed, 2 * j + 1)
                a.activation(hid[:, s % 2, :], g[:, s, 0, :], ACT.Relu).then_inc(hid_set, 1)
                wait(act, z_summed, 2 * j + 2)
                a.activation(hid_hi[:, s % 2, :], g[:, s, 1, :], ACT.Relu).then_inc(hid_set, 1)

            act.wait_ge(B_stored, 16 * NT)
            act.wait_ge(U_stored, 16 * NT)
            evacuate(0, 0)
            over_pairs(act, pair)

            def evacuate_sums(t):
                wait(act, ST_done, t + 1)
                wait(act, u_done, t)
                a.copy(ST[:, :, 0:NP], ps[:, 0, :].rearrange("p (c n) -> p c n", n=128)[:, :, 0:NP]).then_inc(ST_set, 1)

            def store(t):
                wait(act, o_set, t + 1)
                act.dma_start(out.rearrange("(t p) d -> p t d", p=NP)[:, ds(t, 1), :],
                              o_sb.rearrange("p (t d) -> p t d", t=1)).then_inc(o_stored, 16)

            def finish(t, r, n):
                if not is_last(t, NT - 1):
                    evacuate_sums(t + 1)
                wait(act, u_summed, t + 1)
                wait(act, o_done, t - 1)
                a.activation(U_t[:, r, :], U_all[:, ds(KH * NP * t, KH * NP)], ACT.Relu).then_inc(u_set, 1)
                if not (isinstance(t, int) and t == 0):
                    store(t - 1)

            evacuate_sums(0)
            over_blocks(act, finish)
            store(NT - 1)
            act.wait_ge(o_stored, 16 * NT)

        @block.vector
        def _(dve):
            v = nc.vector
            steps = [0]

            def link(ins):
                steps[0] += 1
                ins.then_inc(chain, 1)
                dve.wait_ge(chain, steps[0])

            dve.wait_ge(zero_set, 1)
            dve.wait_ge(iota_set, 3)
            dve.wait_ge(ids_loaded, 32)
            link(v.tensor_copy(local1, src_i))
            link(v.tensor_scalar(bucket, local1, 1.0 / NP, -(NP // 2) / NP, ALU.mult, ALU.add))
            link(v.tensor_scalar_add(bucket, bucket, ROUND))
            link(v.tensor_scalar_add(bucket, bucket, -ROUND))
            cols0, cum, cnt, pairs, ends, base = (small[:, k, :] for k in range(6))
            link(v.tensor_scalar_add(cols0, iota1[0:NP, 0:NT], -1.0))
            link(v.tensor_tensor(hot, bucket.rearrange("p (o c) -> p o c", o=1).to_broadcast([NP, NT, EC]),
                                 cols0.rearrange("p (a o) -> p a o", o=1).to_broadcast([NP, NT, EC]), ALU.is_equal))
            v.tensor_scalar(before, iota1[0:NP, 0:NP], part1[0:NP, :], None, ALU.is_gt)
            v.memset(epsc[:, :], EPS)
            v.memset(ones[:, :], 1.0)
            link(v.tensor_tensor_scan(run_f, hot_f, hot_f, 0.0, ALU.add, ALU.max))
            link(v.tensor_copy(cum, run[:, :, EC - 1:EC].rearrange("p a o -> p (a o)")))
            link(v.tensor_copy(cnt[:, 0:1], cum[:, 0:1]))
            v.tensor_tensor(cnt[:, 1:NT], cum[:, 1:NT], cum[:, 0:NT - 1], ALU.subtract).then_inc(counts_set, 1)
            v.tensor_copy(iotab[:, :], iota1[:, :])
            for m in (ident, identb):
                v.tensor_scalar(m[:, :], iota1[:, :], part1[:, :], None, ALU.is_equal)
            link(v.tensor_scalar_add(local1, local1, 1.0))
            v.scalar_tensor_tensor(local1, bucket, -float(NP), local1, ALU.mult, ALU.add).then_inc(const_set, 1)
            dve.wait_ge(counts_summed, 1)
            tot_ps, bef_ps = ps[0:NP, 0, 0:NT], ps[0:NP, 1, 0:NT]
            link(v.tensor_scalar_add(small_i, tot_ps, float(PAIR - 1)))
            link(v.tensor_scalar(small_i, small_i, 8, None, ALU.logical_shift_right))
            link(v.tensor_copy(pairs, small_i))
            link(v.tensor_tensor_scan(ends, pairs, pairs, 0.0, ALU.add, ALU.max))
            link(v.scalar_tensor_tensor(to_spare, cols0[0:1, :], NPAIR + 1.0, ends[0:1, :], ALU.add, ALU.subtract))
            link(v.scalar_tensor_tensor(to_spare, pairs[0:1, :], 0.0, to_spare, ALU.is_equal, ALU.mult))
            v.scalar_tensor_tensor(last_pair[:, :], ends[0:1, :], -1.0, to_spare, ALU.add, ALU.add
                                   ).then_inc(last_pair_set, 1)
            link(v.tensor_tensor(base, ends, pairs, ALU.subtract))
            link(v.scalar_tensor_tensor(base, base, float(PAIR), bef_ps, ALU.mult, ALU.add))
            v.tensor_scalar_add(base, base, -1.0).then_inc(order_started, 1)
            dve.wait_ge(order_started, 1)
            link(v.tensor_tensor(base[:, 1:NT], base[:, 1:NT], cum[:, 0:NT - 1], ALU.subtract))

            def places(c0, c1):
                c, w = slice(c0, c1), c1 - c0
                link(v.tensor_tensor(run[:, :, c], run[:, :, c],
                                     base.rearrange("p (a o) -> p a o", o=1).to_broadcast([NP, NT, w]), ALU.add))
                link(v.tensor_tensor(run[:, :, c], run[:, :, c], hot[:, :, c], ALU.mult))
                link(v.tensor_reduce(place_f[:, c], run[:, :, c].rearrange("p a c -> p c a"), AX.X, ALU.add))
                link(v.tensor_copy(src_i[:, c], place_f[:, c]))
                link(v.tensor_scalar(place[:, c], src_i[:, c], 127, None, ALU.bitwise_and))
                link(v.tensor_scalar(src_i[:, c], src_i[:, c], 7, None, ALU.logical_shift_right))
                link(v.scalar_tensor_tensor(place[:, c], place[:, c], float(NTILE), src_i[:, c], ALU.mult, ALU.add))

            places(0, FIRST * BC)

            def ended_buckets():
                link(v.tensor_tensor(ends_diag, ends[0:NT, :], ident[0:NT, 0:NT], ALU.mult))
                link(v.tensor_reduce(ends_diag[:, 0:1], ends_diag, AX.X, ALU.add))
                v.tensor_scalar(ended, pair_iota, ends_diag[:, 0:1], None, ALU.is_ge).then_inc(ended_set, 1)

            def split_edge_weights():
                dve.wait_ge(we_loaded, 16)
                link(v.tensor_copy(we[1], we[0]))
                link(v.tensor_tensor(we[0], we[0], we[1], ALU.subtract))
                link(v.tensor_copy(we[2], we[0]))
                v.tensor_tensor(we[3], we[0], we[2], ALU.subtract).then_inc(we_split, 1)

            def build(t, r, n):
                slots = recb_bf[:, r, :, 4:].rearrange("p c (k d) -> p c k d", d=DE)
                e = ea[:, r, :, :]
                wait(dve, scattered[r], 16 * BC * n)
                cols = ds(BC * t, BC)
                v.tensor_copy(recb_i[:, r, :, 0], dst_i[:, cols])
                v.tensor_copy(recb[:, r, :, 1], local1[:, cols])
                v.tensor_copy(row_i[:, r, :], place[:, cols])
                wait(dve, e1_set, t + 1)
                v.tensor_tensor(e, e, slots[:, :, 0, :], ALU.subtract).then_inc(r1_set, 1)
                wait(dve, e2_set, t + 1)
                v.tensor_tensor(
                    slots[:, :, 6:8, :], e.rearrange("p c (o d) -> p c o d", o=1).to_broadcast([NP, BC, 2, DE]),
                    slots[:, :, 3:4, :].to_broadcast([NP, BC, 2, DE]), ALU.subtract).then_inc(rec_built, 1)

            def low_A(t):
                wait(dve, A_hi_set, t + 1)
                v.tensor_tensor(A_lo[:, ds(t, 1), :], ps[0:NP, 2:3, :], A_hi[:, ds(t, 1), :].bitcast(f32),
                                ALU.subtract).then_inc(A_lo_set, 1)

            def step(t, r, n):
                next_build(build, t, r, n)
                if isinstance(t, int) and t == 0:
                    split_edge_weights()
                else:
                    low_A(t - 1)
                if isinstance(t, int) and t == NT - 1:
                    v.memset(S_flat[:, zero_from:zero_from + 4 * EC], 0.0)
                cols = ds(BC * t, BC)
                if isinstance(t, int) and t == 0:
                    dve.wait_ge(upd_done, KH)
                    dve.wait_ge(x_loaded, 16)
                    dve.wait_ge(ub2_done, 1)
                    dve.wait_ge(buckets_counted, 1)
                    link(v.tensor_copy(ub2_rows, ps[0:NP, 7, 0:D]))
                    v.tensor_copy(pair_bucket[:, :], ps[0:1, 6, 0:NPAIR]).then_inc(order_done, 1)
                if not (isinstance(t, int) and t < 2):
                    wait(dve, xh_stored[r], 16 * n)
                    v.tensor_copy(x_all[:, ds(t - 2, 1), :], zero[0:NP, 0:D].rearrange("p (t d) -> p t d", t=1))
                xt = x_all[:, ds(t, 1), :].rearrange("p t d -> p (t d)")
                v.bn_stats(stat[:, 0:6], xt).then_inc(norm_step, 1)
                wait(dve, norm_step, 3 * t + 1)
                dve.nop(nofuse=True)
                v.bn_aggr(stat[:, 6:8], stat[:, 0:6]).then_inc(norm_step, 1)
                wait(dve, std_set, t + 1)
                v.reciprocal(stat[:, 9:10], stat[:, 8:9]).then_inc(norm_step, 1)
                wait(dve, norm_step, 3 * t + 3)
                wait(dve, hT_done, t)
                v.tensor_scalar(h_t, xt, stat[:, 6:7], stat[:, 9:10], ALU.subtract, ALU.mult).then_inc(h_set, 1)
                wait(dve, h_set, 2 * t + 1)
                v.tensor_scalar_max(h_t, h_t, 0.0).then_inc(h_set, 1)
                wait(dve, h_set, 2 * t + 2)
                v.tensor_tensor(xt, xt, h_t, ALU.add).then_inc(xh_set, 1)
                wait(dve, xh_set, 2 * t + 1)
                v.tensor_tensor(xt, xt, ub2_rows, ALU.add).then_inc(xh_set, 1)
                wait(dve, hot_used, t)
                v.tensor_tensor(hot_b, bucket[:, cols].rearrange("p (c o) -> p c o", o=1).to_broadcast([NP, BC, NT]),
                                cols0.rearrange("p (o a) -> p o a", o=1).to_broadcast([NP, BC, NT]), ALU.is_equal)
                v.tensor_tensor(hot_n, local1[:, cols].rearrange("p (c o) -> p c o", o=1).to_broadcast([NP, BC, NP]),
                                iota1[0:NP, 0:NP].rearrange("p (o n) -> p o n", o=1).to_broadcast([NP, BC, NP]),
                                ALU.is_equal).then_inc(hot_set, 1)

            build(0, 0, 0)
            build(1, 1, 0)
            ended_buckets()
            places(FIRST * BC, EC)
            over_blocks(dve, step)
            low_A(NT - 1)

            dve.wait_ge(hot_used, NT)
            v.tensor_copy(cnt_sb, ps[0:NP, 5, 0:NT]).then_inc(cnt_set, 1)
            dve.wait_ge(cntT_done, 1)
            v.tensor_copy(cntT_sb, ps[0:NT, 4, 0:NP]).then_inc(cntT_set, 1)
            dve.wait_ge(U_done, NT)
            dve.wait_ge(order_done, 1)
            dve.wait_ge(we_placed, 16 * NSLOT)
            v.memset(S_flat[:, zero_from + 4 * EC:], 0.0)
            for r in range(2):
                dve.wait_ge(xh_stored[r], 16 * (NT // 2 + 1 - r))
            dve.wait_ge(cnt_stored, 16)
            v.memset(S_flat[:, (NT - 2) * D:zero_from], 0.0).then_inc(S_zeroed, 1)
            dve.wait_ge(S_zeroed, 1)
            dve.wait_ge(upd_stored[1], 16 * (KH // 2))

            def one_hots(j, s, n):
                wait(dve, rec_loaded[s], 16 * n + 16)
                wait(dve, transposed, j - RING + 1)
                wait(dve, hid_set, 2 * (j - RING) + 1)
                v.tensor_tensor(selb[:, s, :, :], iotab[:, :].rearrange("p (o n) -> p o n", o=1).to_broadcast([128, 2, 128]),
                                rec_bf[:, s, :, 3:4].to_broadcast([128, 2, 128]), ALU.is_equal).then_inc(selb_set, 1)

            def bucket_of(j):
                return v.value_load(pair_bucket[0:1, ds(j, 1)], min_val=0, max_val=NT - 1)

            def add_sums(j, s, k):
                row = S[0:NP, ds(k, 1), :].rearrange("p t w -> p (t w)")
                wait(dve, pair_done, j + 1)
                wait(dve, S_added, j)
                v.tensor_tensor(row, row, S_ps[s % 2], ALU.add).then_inc(S_added, 1)

            def pair(j, s, n):
                first = isinstance(j, int) and j == 0
                k = None if first else bucket_of(j - 1)
                for u in range(2):
                    wait(dve, gathered[s][u], 16 * n + 16)
                    wait(dve, z_done, 2 * j + u + 1)
                    v.tensor_tensor(g[:, s, u, :], z_ps[:, u, :], g[:, s, u, :], ALU.add).then_inc(z_summed, 1)
                if not first:
                    add_sums(j - 1, (s - 1) % RING, k)
                if not is_last(j, NPAIR - AHEAD):
                    one_hots(j + AHEAD, (s + AHEAD) % RING, n + (s + AHEAD) // RING)
                wait(dve, hid_set, 2 * j + 2)
                v.scalar_tensor_tensor(hid_lo[:, s % 2, :], g[:, s, 1, :], 0.0, hid_hi[:, s % 2, :].bitcast(f32),
                                       ALU.max, ALU.subtract).then_inc(lo_set, 1)

            for j in range(AHEAD):
                one_hots(j, j, 0)
            over_pairs(dve, pair)
            add_sums(NPAIR - 1, RING - 1, bucket_of(NPAIR - 1))

            dve.wait_ge(S_added, NPAIR)
            dve.wait_ge(hid_set, 2 * NPAIR)
            dve.wait_ge(lo_set, NPAIR)

            def stage(t):
                wait(dve, ST_done, t)
                v.tensor_copy(S_t, S[0:NP, ds(t, 1), :].rearrange("p t w -> p (t w)")).then_inc(S_t_set, 1)

            def output(t):
                wait(dve, o_done, t + 1)
                wait(dve, o_stored, 16 * t)
                v.tensor_tensor(o_sb, ps[0:NP, 4, 0:D], xh_all[:, ds(D * t, D)], ALU.add).then_inc(o_set, 1)

            def finish(t, r, n):
                if not is_last(t, NT - 1):
                    stage(t + 1)
                wait(dve, late_loaded[r], 48 * n + 48)
                for c in range(KH):
                    U = U_all[:, ds(KH * NP * t + c * NP, NP)]
                    last = v.scalar_tensor_tensor(U, cnt_rows[:, ds(NP * t, NP)], q_upd[:, c:c + 1], U,
                                                  ALU.mult, ALU.add)
                last.then_inc(node_step, 1)
                wait(dve, node_step, t + 1)
                wait(dve, u_done, t + 1)
                U = U_all[:, ds(KH * NP * t, KH * NP)]
                v.tensor_tensor(U, ps[:, 3, 0:KH * NP], U, ALU.add).then_inc(u_summed, 1)
                if not (isinstance(t, int) and t == 0):
                    output(t - 1)

            stage(0)
            over_blocks(dve, finish)
            output(NT - 1)

        @block.tensor
        def _(pe):
            mm = nc.tensor.matmul
            pe.wait_ge(counts_set, 1)
            cnt = small[:, 2, :]
            mm(ps[0:NP, 0, 0:NT], ones[0:NP, 0:NP], cnt, start=True, stop=True)
            mm(ps[0:NP, 1, 0:NT], before, cnt, start=True, stop=True).then_inc(counts_summed, 1)
            pe.wait_ge(const_set, 1)
            pe.wait_ge(w3_loaded, 16 * (2 + KD))
            for k in range(KD):
                for c in range(KH):
                    last = nc.tensor.transpose(ps[:, 4 + k, c * 128:(c + 1) * 128],
                                               w_msg2[:, c, k * 128:(k + 1) * 128], ident[:, :])
            last.then_inc(m2T_done, 1)
            for c in range(KH):
                for k in range(KD):
                    mm(ps[:, 6, c:c + 1], w_agg[:, k, c * 128:(c + 1) * 128], mb2_cols[:, k:k + 1],
                       start=k == 0, stop=k == KD - 1)
            pe.wait_ge(m2T_set, 1)
            pe.wait_ge(order_started, 1)
            for c in range(KH):
                for k in range(KD):
                    last = mm(ps[:, c, :], m2T[:, k, c * 128:(c + 1) * 128], w_agg[:, k, :],
                              start=k == 0, stop=k == KD - 1)
                last.then_inc(upd_done, 1)
            pe.wait_ge(q_set, 1)
            pe.wait_ge(w_loaded, 16 * 6)
            mm(ps[0:NP, 7, 0:D], ones[0:1, 0:NP], bias_out, start=True, stop=True).then_inc(ub2_done, 1)
            pe.wait_ge(ended_set, 1)
            mm(ps[0:1, 6, 0:NPAIR], ones[0:NT - 1, 0:1], ended[0:NT - 1, :], start=True, stop=True
               ).then_inc(buckets_counted, 1)

            def step(t, r, n):
                wait(pe, h_set, 2 * t + 2)
                wait(pe, hT_set, t)
                for k in range(KD):
                    last = nc.tensor.transpose(ps[:, 0, k * 128:k * 128 + NP], h_t[:, k * 128:(k + 1) * 128],
                                               ident[0:NP, 0:NP])
                last.then_inc(hT_done, 1)
                wait(pe, hT_set, t + 1)
                wait(pe, B_set, t)
                for k in range(KD):
                    last = mm(ps[0:NP, 1, :], hT[:, k, 0:NP], w_dst[:, k, :], start=k == 0, stop=k == KD - 1)
                last.then_inc(B_done, 1)
                wait(pe, A_lo_set, t)
                for k in range(KD):
                    mm(ps[0:NP, 2, :], hT[:, k, 0:NP], w_src[:, k, :], start=k == 0, stop=False)
                mm(ps[0:NP, 2, :], ones[0:1, 0:NP], bias1[:, 0:H], start=False, stop=True).then_inc(A_done, 1)
                wait(pe, U_set, t)
                for c in range(KH):
                    o = ps[:, 3, c * NP:(c + 1) * NP]
                    for k in range(KD):
                        mm(o, w_node[:, k, c * 128:(c + 1) * 128], hT[:, k, 0:NP], start=k == 0, stop=False)
                    last = mm(o, bias1[:, H + c * 128:H + (c + 1) * 128], ones[0:1, 0:NP], start=False, stop=True)
                last.then_inc(U_done, 1)
                wait(pe, hot_set, t + 1)
                for k in range(BC):
                    first = isinstance(t, int) and t == 0 and k == 0
                    end = is_last(t, NT - 1) and k == BC - 1
                    last = mm(ps[0:NP, 5, 0:NT], hot_n[:, k, :], hot_b[:, k, :], start=first, stop=end,
                              skip_group_check=True)
                last.then_inc(hot_used, 1)

            over_blocks(pe, step)
            pe.wait_ge(we_placed, 16 * NSLOT)
            pe.wait_ge(order_done, 1)
            pe.wait_ge(cnt_set, 1)
            pe.wait_ge(B_set, NT)
            pe.wait_ge(A_lo_set, NT)
            pe.wait_ge(U_set, NT)
            nc.tensor.transpose(ps[0:NT, 4, 0:NP], cnt_sb, ident[0:NP, 0:NP]).then_inc(cntT_done, 1)
            def transposes(j, s):
                wait(pe, selb_set, j + 1)
                wait(pe, lhs_set, j - 1)
                for u in range(2):
                    nc.tensor.transpose(tr_ps[s % 2][:, u, :], selb[:, s, u, :], identb[:, :])
                    last = nc.tensor.transpose(tr_ps[s % 2][:, 2 + u, :], rec_bf[:, s, u, 4:], identb[:, :])
                last.then_inc(transposed, 1)

            def pre_relu(j, s, u, k):
                wait(pe, lhs_set, j + 1)
                wait(pe, z_summed, 2 * (j - 1) + u + 1)
                b = s % 2
                for n, part in enumerate((A_hi, A_lo)):
                    mm(z_ps[:, u, :], selT[0:NP, b, u, :], part[:, ds(k, 1), :].rearrange("p t h -> p (t h)"),
                       start=n == 0, stop=False)
                mm(z_ps[:, u, :], eT[:, b, u, :], w_edge[:, :], start=False, stop=True).then_inc(z_done, 1)

            def sums(j, s, u):
                wait(pe, hid_set, 2 * j + u + 1)
                b = s % 2
                if u == 0:
                    wait(pe, S_added, j - 1)
                    mm(S_ps[b], sel[:, b, 0, 0:NP].bitcast(f32), hid[:, b, :], start=True, stop=False)
                else:
                    wait(pe, lo_set, j + 1)
                    mm(S_ps[b], sel[:, b, 1, 0:NP], hid_hi[:, b, :], start=False, stop=False)
                    mm(S_ps[b], sel[:, b, 1, 0:NP], hid_lo[:, b, :], start=False, stop=True).then_inc(pair_done, 1)

            def pair(j, s, n):
                first = isinstance(j, int) and j == 0
                k = nc.tensor.value_load(pair_bucket[0:1, ds(j, 1)], min_val=0, max_val=NT - 1)
                if not (isinstance(j, int) and j < 2):
                    sums(j - 2, (s - 2) % RING, 1)
                pre_relu(j, s, 0, k)
                if not is_last(j, NPAIR - 1):
                    transposes(j + 1, (s + 1) % RING)
                if not first:
                    sums(j - 1, (s - 1) % RING, 0)
                pre_relu(j, s, 1, k)

            pe.wait_ge(cntT_set, 1)
            transposes(0, 0)
            over_pairs(pe, pair)
            sums(NPAIR - 2, RING - 2, 1)
            for u in range(2):
                sums(NPAIR - 1, RING - 1, u)

            pe.wait_ge(upd_loaded, 32)

            def transpose_sums(t):
                wait(pe, S_t_set, t + 1)
                wait(pe, ST_set, t)
                for c in range(KH):
                    last = nc.tensor.transpose(ps[:, 0, c * 128:c * 128 + NP], S_t[:, c * 128:(c + 1) * 128],
                                               ident[0:NP, 0:NP])
                last.then_inc(ST_done, 1)

            def output(t, r):
                wait(pe, u_set, t + 1)
                wait(pe, o_set, t)
                for c in range(KH):
                    last = mm(ps[0:NP, 4, 0:D], U_t[:, r, c * NP:(c + 1) * NP], w_out[:, c, :],
                              start=c == 0, stop=c == KH - 1)
                last.then_inc(o_done, 1)

            def finish(t, r, n):
                wait(pe, ST_set, t + 1)
                wait(pe, u_summed, t)
                for c in range(KH):
                    for k in range(KH):
                        last = mm(ps[:, 3, c * NP:(c + 1) * NP], w_upd[:, k, c * 128:(c + 1) * 128], ST[:, k, 0:NP],
                                  start=k == 0, stop=k == KH - 1)
                last.then_inc(u_done, 1)
                if not is_last(t, NT - 1):
                    transpose_sums(t + 1)
                if not (isinstance(t, int) and t == 0):
                    output(t - 1, 1 - r)

            transpose_sums(0)
            over_blocks(pe, finish)
            output(NT - 1, (NT - 1) % 2)


_INS = ['x', 'src', 'dst', 'edge_attr_16', 'L0_gnn_mW1', 'L0_gnn_mb1', 'L0_gnn_mW2', 'L0_gnn_mb2', 'L0_gnn_uW1',
        'L0_gnn_ub1', 'L0_gnn_uW2', 'L0_gnn_ub2']


def kernel(**inputs):
    import numpy as _np
    import concourse.bacc as _bacc
    from concourse import mybir as _mybir
    from concourse.bass_utils import run_bass_kernel_spmd as _run

    nc = _bacc.Bacc("TRN2", target_bir_lowering=False, num_devices=1)
    arrays, args = {}, []
    for name in _INS:
        a = _np.ascontiguousarray(inputs[name])
        arrays[f"in_{name}_dram"] = a
        args.append(nc.dram_tensor(f"in_{name}_dram", a.shape, _mybir.dt.from_np(a.dtype), kind="ExternalInput").ap())
    shape = inputs['x'].shape
    args.append(nc.dram_tensor("out_dram", shape, _mybir.dt.float32, kind="ExternalOutput").ap())
    gnn_layer_kernel(nc, *args)
    r = _run(nc, [arrays], core_ids=[0])
    return r.results[0]["out_dram"]
```
